# Optimizing a Trainium2 kernel written in Bass

```python
import numpy as np
import jax
import jax.numpy as jnp

def _softmax(x, axis=-1):
    return jax.nn.softmax(x, axis=axis)

def _gelu(x):
    return jax.nn.gelu(x, approximate=True)

def _silu(x):
    return jax.nn.silu(x)

def _sigmoid(x):
    return jax.nn.sigmoid(x)

def _layernorm(x, axis=-1, eps=1e-05):
    m = jnp.mean(x, axis=axis, keepdims=True)
    v = jnp.var(x, axis=axis, keepdims=True)
    return (x - m) / jnp.sqrt(v + eps)

def _scatter_add(tgt, idx, src, axis=0):
    return tgt.at[idx].add(src)

def _segment_sum(src, seg, n):
    return jax.ops.segment_sum(src, seg, n)
kernel_name = 'mk_cond_resid_d2_seqx_r4_60f772'

def setup_inputs(seed: int=0):
    np.random.seed(seed)
    _w = jnp.asarray

    def _rec_inputs():
        import jax
        import jax.numpy as jnp
        _rk = jax.random.key(seed)
        x = -0.0003929 + 0.9999 * jax.random.normal(jax.random.fold_in(_rk, 1), (4, 512, 512), jnp.float32)
        _lenS = 512 - jax.random.randint(jax.random.fold_in(_rk, 7), (4,), 0, max(1, 512 // 4) + 1, jnp.int32)
        _lenS2 = 512 - jax.random.randint(jax.random.fold_in(_rk, 8), (4,), 0, max(1, 512 // 4) + 1, jnp.int32)
        cond_2048 = 0.00782532 + 1.00527 * jax.random.normal(jax.random.fold_in(_rk, 11), (4, 512), jnp.float32)
        return (x, cond_2048)
    x, cond_2048 = _rec_inputs()

    def _L0_cond_setup():
        import jax, jax.numpy as jnp
        import numpy as np
        HEADS = 16
        EPS = 1e-06

        def _rms_norm(x, g):
            xf = x.astype(jnp.float32)
            y = xf * jax.lax.rsqrt(jnp.mean(xf * xf, axis=-1, keepdims=True) + EPS)
            return y.astype(x.dtype) * g
        key = jax.random.key(seed)
        ks = jax.random.split(key, 6)
        b, n, dim, emb_dim = (4, 512, 512, 512)
        d_head = dim // HEADS
        return {'x': jax.random.normal(ks[0], (b, n, dim), jnp.float32), 'emb': jax.random.normal(ks[1], (b, 1, emb_dim), jnp.float32), 'W_emb': jax.random.normal(ks[2], (emb_dim, 2 * dim), jnp.float32) * emb_dim ** (-0.5), 'b_emb': jnp.zeros((2 * dim,), jnp.float32), 'g_norm': jnp.ones((dim,), jnp.float32), 'W_qkv': jax.random.normal(ks[3], (dim, 3 * dim), jnp.float32) * dim ** (-0.5), 'g_q': jnp.ones((d_head,), jnp.float32), 'g_k': jnp.ones((d_head,), jnp.float32), 'W_out': jax.random.normal(ks[4], (dim, dim), jnp.float32) * dim ** (-0.5)}
    _L0_cond_all = _L0_cond_setup()
    _L0_cond_in = {k: v for k, v in _L0_cond_all.items() if k in ('W_emb', 'b_emb', 'g_norm', 'W_qkv', 'g_q', 'g_k', 'W_out')}
    del _L0_cond_all

    def _L1_cond_setup():
        import jax, jax.numpy as jnp
        import numpy as np
        B, T, D = (16, 128, 512)
        key = jax.random.key(seed)
        k0, k1, k2, k3 = jax.random.split(key, 4)
        scale = 1.0 / np.sqrt(D)
        return {'initial_state': jax.random.normal(k0, (B, D), jnp.float32), 'inputs': jax.random.normal(k1, (B, T, D), jnp.float32), 'W_ih': jax.random.normal(k2, (D, 3 * D), jnp.float32) * scale, 'W_hh': jax.random.normal(k3, (D, 3 * D), jnp.float32) * scale, 'b_ih': jnp.zeros((3 * D,), jnp.float32), 'b_hh': jnp.zeros((3 * D,), jnp.float32)}
    _L1_cond_all = _L1_cond_setup()
    _L1_cond_in = {k: v for k, v in _L1_cond_all.items() if k in ('W_ih', 'W_hh', 'b_ih', 'b_hh')}
    del _L1_cond_all
    return {'x': x, 'cond_2048': cond_2048, 'L0_cond_W_emb': _L0_cond_in['W_emb'], 'L0_cond_b_emb': _L0_cond_in['b_emb'], 'L0_cond_g_norm': _L0_cond_in['g_norm'], 'L0_cond_W_qkv': _L0_cond_in['W_qkv'], 'L0_cond_g_q': _L0_cond_in['g_q'], 'L0_cond_g_k': _L0_cond_in['g_k'], 'L0_cond_W_out': _L0_cond_in['W_out'], 'L1_cond_W_ih': _L1_cond_in['W_ih'], 'L1_cond_W_hh': _L1_cond_in['W_hh'], 'L1_cond_b_ih': _L1_cond_in['b_ih'], 'L1_cond_b_hh': _L1_cond_in['b_hh']}

def reference(x, cond_2048, L0_cond_W_emb, L0_cond_b_emb, L0_cond_g_norm, L0_cond_W_qkv, L0_cond_g_q, L0_cond_g_k, L0_cond_W_out, L1_cond_W_ih, L1_cond_W_hh, L1_cond_b_ih, L1_cond_b_hh):
    import jax
    import jax.numpy as jnp

    def _L0_cond_ref(x, emb, W_emb, b_emb, g_norm, W_qkv, g_q, g_k, W_out):
        import jax, jax.numpy as jnp
        import numpy as np
        HEADS = 16
        EPS = 1e-06

        def _rms_norm(x, g):
            xf = x.astype(jnp.float32)
            y = xf * jax.lax.rsqrt(jnp.mean(xf * xf, axis=-1, keepdims=True) + EPS)
            return y.astype(x.dtype) * g
        b, n, dim = x.shape
        h = HEADS
        d = dim // h
        scale_shift = emb @ W_emb + b_emb
        scale, shift = jnp.split(scale_shift, 2, axis=-1)
        xn = _rms_norm(x, g_norm) * (1.0 + scale) + shift
        qkv = xn @ W_qkv
        qkv = qkv.reshape(b, n, 3, h, d)
        q, k, v = jnp.moveaxis(qkv, 2, 0)
        q = jnp.swapaxes(q, 1, 2)
        k = jnp.swapaxes(k, 1, 2)
        v = jnp.swapaxes(v, 1, 2)
        q = _rms_norm(q, g_q)
        k = _rms_norm(k, g_k)
        logits = jnp.einsum('bhqd,bhkd->bhqk', q, k) * d ** (-0.5)
        attn = jax.nn.softmax(logits, axis=-1)
        o = jnp.einsum('bhqk,bhkd->bhqd', attn, v)
        o = jnp.swapaxes(o, 1, 2).reshape(b, n, dim)
        return o + o @ W_out

    def _L1_cond_ref(initial_state, inputs, W_ih, W_hh, b_ih, b_hh):
        import jax, jax.numpy as jnp
        import numpy as np
        B, T, D = (16, 128, 512)
        "ScanOverTime(GRU cell): sequential per-timestep module call with\n            dict-state passing; merge_dict_trees stacks the per-step\n            'state_predicted' tensors along axis=1 -> [B, T, D]."

        def cell(h, x):
            gi = x @ W_ih + b_ih
            gh = h @ W_hh + b_hh
            i_r, i_z, i_n = jnp.split(gi, 3, axis=-1)
            h_r, h_z, h_n = jnp.split(gh, 3, axis=-1)
            r = jax.nn.sigmoid(i_r + h_r)
            z = jax.nn.sigmoid(i_z + h_z)
            n = jnp.tanh(i_n + r * h_n)
            h_new = (1.0 - z) * n + z * h
            return (h_new, h_new)
        xs = jnp.swapaxes(inputs, 0, 1)
        _, hs = jax.lax.scan(cell, initial_state, xs)
        return jnp.swapaxes(hs, 0, 1)
    x = x + _L0_cond_ref(x, cond_2048[:, None, :], L0_cond_W_emb, L0_cond_b_emb, L0_cond_g_norm, L0_cond_W_qkv, L0_cond_g_q, L0_cond_g_k, L0_cond_W_out)
    x = x + _L1_cond_ref(cond_2048, x, L1_cond_W_ih, L1_cond_W_hh, L1_cond_b_ih, L1_cond_b_hh)
    return x

_drawn_inputs = setup_inputs


def setup_inputs(seed=0):
    import zlib

    import numpy as np

    out = dict(_drawn_inputs(seed))
    spreads = {'L0_cond_b_emb': (0.0, 0.1),
     'L0_cond_g_norm': (1.0, 0.2),
     'L0_cond_g_q': (1.0, 0.6),
     'L0_cond_g_k': (1.0, 0.6),
     'L1_cond_b_ih': (0.0, 0.309),
     'L1_cond_b_hh': (0.0, 0.496)}
    factors = {}
    for name, (base, spread) in spreads.items():
        noise = np.random.default_rng([zlib.crc32(name.encode()), seed]).standard_normal(out[name].shape)
        drawn = base * np.exp(spread * noise) if base else spread * noise
        out[name] = jnp.asarray(drawn.astype(out[name].dtype))
    for name, factor in factors.items():
        out[name] = (out[name] * factor).astype(out[name].dtype)
    return out
```

```python
from contextlib import ExitStack

import concourse.bass as bass
from concourse import mybir

ALU = mybir.AluOpType
ACT = mybir.ActivationFunctionType
F32 = mybir.dt.float32
AX_X = mybir.AxisListType.X

P = 128
B, T, D = 4, 512, 512
HEADS = 16
DH = D // HEADS
KT = D // P
TT = T // P
G = HEADS // 4
EPS = 1e-6
BLK = P // B
QD = 32
N_TILES = G * TT
N_QUADS = G * TT
LAG = 5
N_SLOTS = N_QUADS + LAG + 1


def attention_gru_kernel(nc, x, cond, W_emb, b_emb, g_norm, W_qkv, g_q, g_k, W_out,
                         W_ih, W_hh, b_ih, b_hh, out):
    with ExitStack() as ctx:
        def sb(name, shape):
            return ctx.enter_context(nc.sbuf_tensor(name, shape, F32))

        def sem(name):
            return ctx.enter_context(nc.semaphore(name))

        wqkv = sb("wqkv", [P, KT, 3 * D])
        wout = sb("wout", [P, KT, D])
        wih = sb("wih", [P, KT, 3 * D])
        whh = sb("whh", [P, KT, 3 * D])
        ident = sb("ident", [P, P])
        gq_s = sb("gq_s", [P, 1])
        gk = sb("gk", [P, 1])
        condT = sb("condT", [P, KT, B])
        bembT = sb("bembT", [P, 2 * KT])
        gnT = sb("gnT", [P, KT])
        mod_all = sb("mod_all", [P, B, 2 * KT])
        mod_b = sb("mod_b", [P, 2 * KT])
        brz = sb("brz", [P, 2 * D])
        brz2 = sb("brz2", [P, 2 * D])
        bhn = sb("bhn", [P, D])
        binT = sb("binT", [P, KT])
        half_neg = sb("half_neg", [P, 8])

        x1T = sb("x1T", [P, KT, B, T])
        wemb = x1T[:].rearrange("p k b t -> p (k b t)")[:, 0:KT * 2 * D].rearrange("p (k n) -> p k n", k=KT)

        xb = sb("xb", [P, TT, D])
        xr = sb("xr", [P, TT, D])
        xnT = sb("xnT", [P, KT, T])
        xT = sb("xT", [P, KT, T])
        ssq = sb("ssq", [P, TT])
        ms = sb("ms", [P, TT])
        rstd = sb("rstd", [P, TT])
        sq = sb("sq", [P, 2, 2 * P])
        qk_ss = sb("qk_ss", [P, 2, 8])
        qk_ms = sb("qk_ms", [P, 2, 8])
        qk_rs = sb("qk_rs", [P, 2, 8])
        qn = sb("qn", [P, 2, 2 * P])
        qkT = sb("qkT", [P, 2, 2, T])
        v_sb = sb("v_sb", [P, G, TT, P])
        probs = sb("probs", [P, 4, T])
        probsT = sb("probsT", [P, 4, TT, P])
        negmax = sb("negmax", [P, 2, 4])
        sums = sb("sums", [P, 2, 4])
        rexp = sb("rexp", [P, P])
        rT_sb = sb("rT_sb", [P, T])
        oT = sb("oT", [P, G, T])

        xr_flat = xr[:].rearrange("p a b -> p (a b)")
        xb_flat = xb[:].rearrange("p a b -> p (a b)")
        gi = xr_flat[:, 0:3 * D].rearrange("p (g j n) -> p g j n", g=3, j=4)
        gi_rows = xr_flat[:, 0:3 * D]
        x1_rows = xr_flat[:, 3 * D:4 * D]
        x1_blk = xb_flat[:, 0:D].rearrange("p (c r) -> p c r", c=KT)
        h_blk = xb_flat[:, D:2 * D].rearrange("p (c r) -> p c r", c=KT)
        out_rows = xb_flat[:, 2 * D:3 * D]
        gi_nT = xb_flat[:, 3 * D:4 * D].rearrange("p (t u) -> p t u", t=BLK)
        h_ring = sb("h_ring", [P, BLK, KT * B])
        qT = sb("qT", [P, P])
        t_r = sb("t_r", [P, 16])
        t_z = sb("t_z", [P, 16])
        n_new = sb("n_new", [P, 16])
        w_n = sb("w_n", [P, 16])
        n_plus_h = sb("n_plus_h", [P, 16])
        h_minus_n = sb("h_minus_n", [P, 16])
        z_part = sb("z_part", [P, 16])
        wait_mark = sb("wait_mark", [P, 1])

        ps = ctx.enter_context(nc.psum_tensor("ps", [P, 8, 512], F32))
        SC, PO, PJ, PM = (0, 1, 2, 3), 4, (5, 6), 7
        RQ, Z, RV, ZT, GR, GZ, GN, PH = range(8)
        rT_ps = ps[:, RV, 0:P]
        v_ps = ps[:, RV, P:P + 16]
        zT_ps = ps[:, ZT, 0:P]

        (ld_cond, ld_emb, ld_wqkv, ld_wout, ld_wih, ld_whh, ld_bias, ld_h0, ld_x, ld_g, st_out) = (
            sem(n) for n in ("ld_cond", "ld_emb", "ld_wqkv", "ld_wout", "ld_wih", "ld_whh", "ld_bias",
                             "ld_h0", "ld_x", "ld_g", "st_out"))
        s = {n: sem(n) for n in (
            "ident_zero", "ident_ready", "half_ready", "emb_done", "bemb1", "mod_ready", "gq_ready",
            "ssq_done", "ms_done", "rstd_done", "modb_ready", "xr_ready", "xn_ps", "xnT_ready", "x_ps",
            "xT_ready", "out_sent", "pool_waited",
            "proj_done", "sq_done", "ss_done", "qkms_done", "qkrs_done", "qn_done", "tqk_done", "qkT_ready",
            "s_done", "max_done", "exp_done", "pt_done", "ptev_dve", "ptev_act",
            "rexp_done", "rtr_done", "r_ready", "pv_done", "oT_ready", "ox_ready", "y_done", "x1_ready",
            "brz_ready", "gi_const", "x1blk_ready", "gr_done", "gz_done", "gn_done", "x1r_done",
            "gi_ready", "gin_ready", "x1row_ready", "hblk_ready", "ht_done", "outrow_ready",
            "rq_done", "z_done", "rT_done", "rq_read", "zT_done", "w_done", "v_done",
            "sd_done", "zp_done", "h_ready", "tr_done", "tz_done", "n_done")}

        b4 = lambda ap: ap.rearrange("p (c b) -> p c b", b=B)
        from_block = lambda ap: ap.rearrange("p (c r) -> p c r", r=QD)[:, :, 0:B]

        block = ctx.enter_context(nc.Block())

        @block.sync
        def _(sp):
            nat = lambda w: w.rearrange("(k p) n -> p k n", p=P)
            for k in range(KT):
                sp.dma_start(condT[:, k, :], cond[:, P * k:P * k + P].rearrange("b p -> p b"),
                             allow_slow_non_contiguous=True).then_inc(ld_cond, 16)
            sp.dma_start(bembT[:], b_emb.rearrange("(k p) -> p k", p=P), allow_slow_non_contiguous=True).then_inc(ld_cond, 16)
            sp.dma_start(gnT[:], g_norm.rearrange("(k p) -> p k", p=P), allow_slow_non_contiguous=True).then_inc(ld_cond, 16)
            sp.dma_start(xb[:], x[0].rearrange("(t p) f -> p t f", p=P)).then_inc(ld_x, 16)
            sp.dma_start(wemb, nat(W_emb)).then_inc(ld_emb, 16)
            for hh in range(4):
                sp.dma_start(gq_s[QD * hh:QD * hh + QD, :], g_q.rearrange("(d o) -> d o", o=1)).then_inc(ld_g, 16)
                sp.dma_start(gk[QD * hh:QD * hh + QD, :], g_k.rearrange("(d o) -> d o", o=1)).then_inc(ld_g, 16)
            with sp.Fori(0, B - 1) as b:
                sp.wait_ge(s["xT_ready"], sp.snap(b * KT + KT))
                sp.dma_start(xb[:], x[bass.ds(b + 1, 1), :, :].rearrange("o (t p) f -> p (o t) f", p=P)).then_inc(ld_x, 16)
            with sp.Fori(0, T // BLK) as m:
                sp.wait_ge(s["outrow_ready"], sp.snap(m + 2))
                for b in range(B):
                    sp.dma_start(out[b, bass.ds(m * BLK, BLK), :], out_rows[BLK * b:BLK * b + BLK, :]).then_inc(st_out, 16)
                sp.wait_ge(st_out, sp.snap(m * (16 * B) + 16 * B))
                sp.sem_inc(s["out_sent"], 1)
            sp.wait_ge(st_out, 16 * B * T // BLK)

        @block.gpsimd
        def _(pool):
            def await_on_pool(semaphore, value):
                pool.wait_ge(semaphore, value)
                pool.sem_inc(s["pool_waited"], 1)

            pool.dma_start(wqkv[:], W_qkv.rearrange("(k p) n -> p k n", p=P)).then_inc(ld_wqkv, 16)
            nc.gpsimd.memset(ident[:], 0.0).then_inc(s["ident_zero"], 1)
            pool.wait_ge(s["ident_zero"], 1)
            nc.gpsimd.affine_select(out=ident[:], in_=ident[:], compare_op=ALU.not_equal, fill=1.0, base=0,
                                    pattern=[[-1, P]], channel_multiplier=1).then_inc(s["ident_ready"], 1)
            nc.gpsimd.memset(half_neg[:], -0.5).then_inc(s["half_ready"], 1)
            pool.dma_start(wout[:], W_out.rearrange("(k p) n -> p k n", p=P)).then_inc(ld_wout, 16)
            pool.dma_start(wih[:, :, 0:2 * D], W_ih[:, 0:2 * D].rearrange("(k p) n -> p k n", p=P)).then_inc(ld_wih, 16)
            for k in range(KT):
                for j in range(4):
                    pool.dma_start(
                        wih[:, k, 2 * D:3 * D].rearrange("p (c j x) -> p j c x", c=KT, j=4)[:, j],
                        W_ih[P * k:P * k + P, 2 * D + P * j:2 * D + P * j + P].rearrange("p (c x) -> p c x", c=KT)).then_inc(ld_wih, 16)
            for j in range(4):
                q = slice(QD * j, QD * j + QD)
                pool.dma_start(whh[q, :, :], W_hh[P * j:P * j + P, :].rearrange("(c x) n -> x c n", c=KT)).then_inc(ld_whh, 16)
                for c in range(KT):
                    u0 = P * j + QD * c
                    pool.dma_start(h_ring[q, BLK - 1, B * c:B * c + B], cond[:, u0:u0 + QD].rearrange("b x -> x b"),
                                   allow_slow_non_contiguous=True).then_inc(ld_h0, 16)
                pool.dma_start(binT[q, :], b_ih[2 * D + P * j:2 * D + P * j + P].rearrange("(c x) -> x c", c=KT), allow_slow_non_contiguous=True).then_inc(ld_bias, 16)
            pool.dma_start(brz[:], b_ih[0:2 * D].partition_broadcast(P)).then_inc(ld_bias, 16)
            pool.dma_start(brz2[:], b_hh[0:2 * D].partition_broadcast(P)).then_inc(ld_bias, 16)
            pool.dma_start(bhn[:], b_hh[2 * D:3 * D].partition_broadcast(P)).then_inc(ld_bias, 16)

            pool.wait_ge(s["half_ready"], 1)
            with pool.Fori(0, B) as b:
                b1 = pool.snap(b + 1)
                await_on_pool(s["ssq_done"], b1)
                nc.gpsimd.tensor_scalar(ms[:], ssq[:], 1.0 / D, EPS, ALU.mult, ALU.add).then_inc(s["ms_done"], 1)
                await_on_pool(s["ms_done"], b1)
                nc.gpsimd.tensor_tensor(rstd[:], ms[:], half_neg[:, 0:TT], ALU.pow).then_inc(s["rstd_done"], 1)
                for n in range(N_TILES):
                    n1 = pool.snap(b * N_TILES + (n + 1))
                    await_on_pool(s["ss_done"], n1)
                    nc.gpsimd.tensor_scalar(qk_ms[:, n % 2], qk_ss[:, n % 2], 1.0 / DH, EPS, ALU.mult, ALU.add).then_inc(s["qkms_done"], 1)
                    await_on_pool(s["qkms_done"], n1)
                    nc.gpsimd.tensor_tensor(qk_rs[:, n % 2], qk_ms[:, n % 2], half_neg[:], ALU.pow).then_inc(s["qkrs_done"], 1)
                await_on_pool(s["oT_ready"], pool.snap(b * G + (G + 1)))
                await_on_pool(s["xT_ready"], pool.snap(b * KT + KT))
                nc.gpsimd.tensor_tensor(xT[:].rearrange("p k t -> p (k t)"), xT[:].rearrange("p k t -> p (k t)"),
                                        oT[:].rearrange("p k t -> p (k t)"), ALU.add).then_inc(s["ox_ready"], 1)

            with pool.Fori(0, T // BLK) as m:
                m1 = pool.snap(m + 1)
                await_on_pool(s["x1_ready"], (B + 1) * KT)
                await_on_pool(s["x1r_done"], m1)
                nc.gpsimd.tensor_copy(x1_blk.rearrange("p c (b t) -> p (c b) t", b=B),
                                      x1T[:].rearrange("p c b t -> p (c b) t")[:, :, bass.ds(m * BLK, BLK)]).then_inc(s["x1blk_ready"], 1)
                await_on_pool(s["h_ready"], pool.snap(m * BLK + (BLK + 1)))
                nc.gpsimd.tensor_copy(h_blk.rearrange("p c (b t) -> p (c b) t", b=B),
                                      h_ring[:].rearrange("p t u -> p u t")).then_inc(s["hblk_ready"], 1)

        @block.tensor
        def _(pe):
            def transpose(dst, src):
                return nc.tensor.transpose(dst, src, ident[:])

            pe.wait_ge(s["ident_ready"], 1)
            pe.wait_ge(ld_cond, 16 * (KT + 2))
            pe.wait_ge(ld_emb, 16)
            for c in range(2 * KT):
                for k in range(KT):
                    last = nc.tensor.matmul(ps[:, PM, B * c:B * c + B], wemb[:, k, P * c:P * c + P], condT[:, k, :],
                                            start=(k == 0), stop=(k == KT - 1))
            last.then_inc(s["emb_done"], 1)
            pe.wait_ge(s["mod_ready"], 1)

            with pe.Fori(0, B) as b:
                for c in range(KT):
                    pe.wait_ge(s["x1_ready"], pe.snap(b * KT + (c + 1)))
                    for t in range(TT):
                        if c == 0:
                            pe.wait_ge(s["xr_ready"], pe.snap(b * TT + (t + 1)))
                        last = transpose(ps[:, SC[c], P * t:P * t + P], xr[:, t, P * c:P * c + P])
                    last.then_inc(s["xn_ps"], 1)
                for c in range(KT):
                    pe.wait_ge(s["xnT_ready"], pe.snap(b * KT + (c + 1)))
                    for t in range(TT):
                        last = transpose(ps[:, SC[c], P * t:P * t + P], xb[:, t, P * c:P * c + P])
                    last.then_inc(s["x_ps"], 1)
                pe.wait_ge(ld_wqkv, 16)
                for slot in range(N_SLOTS):
                    n, m = slot, slot - LAG
                    if 0 <= m < N_QUADS:
                        g, q = divmod(m, TT)
                        if q == 0:
                            pe.wait_ge(s["qkT_ready"], pe.snap(b * N_TILES + (TT * g + TT)))
                        for hh in range(4):
                            if m == 0:
                                pe.wait_ge(s["xT_ready"], pe.snap(b * KT + (hh + 1)))
                            elif hh < 2:
                                pe.wait_ge(s["ptev_dve"], pe.snap(b * (2 * N_QUADS) + (2 * m - 1 + hh)))
                            else:
                                pe.wait_ge(s["ptev_act"], pe.snap(b * (2 * N_QUADS) + (2 * m - 3 + hh)))
                            r = slice(QD * hh, QD * hh + QD)
                            nc.tensor.matmul(ps[:, SC[hh], :], qkT[r, g % 2, 0, P * q:P * q + P], qkT[r, g % 2, 1, :],
                                             start=True, stop=True, tile_position=(QD * hh, 0)).then_inc(s["s_done"], 1)
                    if 0 <= m - 1 < N_QUADS:
                        g, q = divmod(m - 1, TT)
                        u1 = b * N_QUADS + m
                        if q == 0:
                            pe.wait_ge(s["oT_ready"], pe.snap(b * G + (g + 1)))
                        pe.wait_ge(s["rexp_done"], pe.snap(u1))
                        pe.wait_ge(s["qkT_ready"], pe.snap(b * N_TILES + min(slot - 1, N_TILES)))
                        transpose(ps[:, PM, 0:P], rexp[:]).then_inc(s["rtr_done"], 1)
                        pe.wait_ge(s["ptev_dve"], pe.snap(b * (2 * N_QUADS) + 2 * m))
                        pe.wait_ge(s["ptev_act"], pe.snap(b * (2 * N_QUADS) + 2 * m))
                        for kc in range(TT):
                            for hh in range(4):
                                last = nc.tensor.matmul(
                                    ps[QD * hh:QD * hh + QD, PO, P * q:P * q + P],
                                    v_sb[:, g, kc, QD * hh:QD * hh + QD], probsT[:, hh, kc, :],
                                    start=(kc == 0), stop=(kc == TT - 1), tile_position=(0, QD * hh))
                        last.then_inc(s["pv_done"], 1)
                    if n < N_TILES:
                        g, t = divmod(n, TT)
                        if n == 0:
                            pe.wait_ge(s["xnT_ready"], pe.snap(b * KT + KT))
                        pe.wait_ge(s["qn_done"], pe.snap(b * N_TILES + (n + 1)))
                        for k in range(KT):
                            last = nc.tensor.matmul(ps[:, PJ[n % 2], 0:3 * P], xnT[:, k, P * t:P * t + P],
                                                    wqkv[:, k, :].rearrange("p (a g n) -> p a g n", a=3, g=G)[:, :, g, :],
                                                    start=(k == 0), stop=(k == KT - 1))
                        last.then_inc(s["proj_done"], 1)
                    if 1 <= n <= N_TILES:
                        pe.wait_ge(s["qn_done"], pe.snap(b * N_TILES + (n + 2)))
                        if n >= 2:
                            pe.wait_ge(s["qkT_ready"], pe.snap(b * N_TILES + (n - 1)))
                        if 0 <= m - 1:
                            pe.wait_ge(s["r_ready"], pe.snap(b * N_QUADS + m))
                        transpose(ps[:, PM, 0:P], qn[:, (n - 1) % 2, 0:P])
                        transpose(ps[:, PM, P:2 * P], qn[:, (n - 1) % 2, P:2 * P]).then_inc(s["tqk_done"], 1)
                    if 0 <= m < N_QUADS:
                        for hh in range(4):
                            pe.wait_ge(s["exp_done"], pe.snap(b * (4 * N_QUADS) + (4 * m + hh + 1)))
                            for kc in range(TT):
                                last = transpose(ps[:, SC[hh], P * kc:P * kc + P], probs[:, hh, P * kc:P * kc + P])
                            last.then_inc(s["pt_done"], 1)
                pe.wait_ge(ld_wout, 16)
                pe.wait_ge(s["oT_ready"], pe.snap(b * G + (G + 1)))
                for c in range(KT):
                    for k in range(KT):
                        last = nc.tensor.matmul(ps[:, SC[c], :], wout[:, k, P * c:P * c + P], oT[:, k, :],
                                                start=(k == 0), stop=(k == KT - 1))
                    last.then_inc(s["y_done"], 1)

            pe.wait_ge(ld_wih, 16 * 17)
            pe.wait_ge(ld_whh, 64)
            pe.wait_ge(ld_h0, 16 * 4 * KT)
            pe.wait_ge(s["gi_const"], 1)
            w_g = lambda k: whh[:, k, :].rearrange("p (g j n) -> p g j n", g=3, j=4)
            with pe.Fori(0, T // BLK) as m:
                m1 = pe.snap(m + 1)
                pe.wait_ge(s["x1blk_ready"], m1)
                pe.wait_ge(s["gi_ready"], m1)
                for bank, gate, done in ((GR, 0, "gr_done"), (GZ, 1, "gz_done")):
                    for k in range(KT):
                        last = nc.tensor.matmul(ps[:, bank, :], x1_blk[:, k, :], wih[:, k, D * gate:D * gate + D],
                                                start=(k == 0), stop=(k == KT - 1))
                    last.then_inc(s[done], 1)
                pe.wait_ge(s["gin_ready"], m1)
                for c in range(KT):
                    for k in range(KT):
                        last = nc.tensor.matmul(ps[:, GN, P * c:P * c + P], wih[:, k, 2 * D + P * c:2 * D + P * c + P],
                                                x1_blk[:, k, :], start=(k == 0), stop=(k == KT - 1))
                last.then_inc(s["gn_done"], 1)
                pe.wait_ge(s["outrow_ready"], m1)
                for c in range(KT):
                    last = transpose(ps[:, PH, P * c:P * c + P], x1_blk[:, c, :])
                last.then_inc(s["x1r_done"], 1)
                pe.wait_ge(s["gi_ready"], pe.snap(m + 2))
                for u in range(BLK):
                    t1 = pe.snap(m * BLK + (u + 1))
                    sel = ident[:, u::BLK]
                    prev = h_ring[:, (u - 1) % BLK, :]
                    pe.wait_ge(s["rq_read"], t1)
                    for j in range(4):
                        nc.tensor.matmul(ps[QD * j:QD * j + B, RQ, 0:2 * P], sel, gi[:, 0:3:2, j, :],
                                         start=True, stop=False, tile_position=(0, QD * j))
                    pe.wait_ge(s["zT_done"], t1)
                    for j in range(4):
                        nc.tensor.matmul(ps[QD * j:QD * j + B, Z, 0:P], sel, gi[:, 1, j, :],
                                         start=True, stop=False, tile_position=(0, QD * j))
                    pe.wait_ge(s["h_ready"], t1)
                    for k in range(KT):
                        for j in range(4):
                            last = nc.tensor.matmul(ps[QD * j:QD * j + B, RQ, 0:2 * P], prev[:, B * k:B * k + B],
                                                    w_g(k)[:, 0:3:2, j, :], start=False, stop=(k == KT - 1),
                                                    tile_position=(0, QD * j))
                    last.then_inc(s["rq_done"], 1)
                    for k in range(KT):
                        for j in range(4):
                            last = nc.tensor.matmul(ps[QD * j:QD * j + B, Z, 0:P], prev[:, B * k:B * k + B],
                                                    w_g(k)[:, 1, j, :], start=False, stop=(k == KT - 1),
                                                    tile_position=(0, QD * j))
                    last.then_inc(s["z_done"], 1)
                pe.wait_ge(s["hblk_ready"], m1)
                pe.wait_ge(s["x1row_ready"], m1)
                for c in range(KT):
                    last = transpose(ps[:, PH, P * c:P * c + P], h_blk[:, c, :])
                last.then_inc(s["ht_done"], 1)

        @block.scalar
        def _(act):
            act.wait_ge(ld_g, 128)
            nc.scalar.mul(gq_s[:], gq_s[:], DH ** -0.5).then_inc(s["gq_ready"], 1)
            with act.Fori(0, B) as b:
                b1 = act.snap(b + 1)
                act.wait_ge(ld_x, act.snap(b * 16 + 16))
                for t in range(TT):
                    last = nc.scalar.activation(probs[:, t, :], xb[:, t, :], ACT.Square, accum_out=ssq[:, t:t + 1])
                last.then_inc(s["ssq_done"], 1)
                for c in range(KT):
                    act.wait_ge(s["x_ps"], act.snap(b * KT + (c + 1)))
                    if c == 0:
                        act.wait_ge(s["x1_ready"], act.snap(b * KT + KT))
                    nc.scalar.activation(xT[:, c, :], ps[:, SC[c], :], ACT.Copy).then_inc(s["xT_ready"], 1)
                act.wait_ge(s["gq_ready"], 1)
                for slot in range(N_SLOTS):
                    n, m = slot, slot - LAG
                    if 0 <= m - 1 < N_QUADS:
                        g, q = divmod(m - 1, TT)
                        act.wait_ge(s["rtr_done"], act.snap(b * N_QUADS + m))
                        nc.scalar.activation(rT_sb[:, P * q:P * q + P], ps[:, PM, 0:P], ACT.Copy).then_inc(s["r_ready"], 1)
                    if 0 <= m < N_QUADS:
                        for hh in range(4):
                            act.wait_ge(s["max_done"], act.snap(b * (4 * N_QUADS) + (4 * m + hh + 1)))
                            nc.scalar.activation(probs[:, hh, :], ps[:, SC[hh], :], ACT.Exp,
                                                 bias=negmax[:, m % 2, hh:hh + 1],
                                                 accum_out=sums[:, m % 2, hh:hh + 1]).then_inc(s["exp_done"], 1)
                    if n < N_TILES:
                        g, t = divmod(n, TT)
                        act.wait_ge(s["proj_done"], act.snap(b * N_TILES + (n + 1)))
                        nc.scalar.activation(v_sb[:, g, t, :], ps[:, PJ[n % 2], 2 * P:3 * P], ACT.Copy)
                        nc.scalar.activation(sq[:, n % 2, :], ps[:, PJ[n % 2], 0:2 * P], ACT.Square).then_inc(s["sq_done"], 1)
                    if 1 <= n <= N_TILES:
                        g, t = divmod(n - 1, TT)
                        act.wait_ge(s["tqk_done"], act.snap(b * N_TILES + n))
                        nc.scalar.activation(qkT[:, g % 2, 0, P * t:P * t + P], ps[:, PM, 0:P], ACT.Copy, scale=gq_s[:])
                        nc.scalar.activation(qkT[:, g % 2, 1, P * t:P * t + P], ps[:, PM, P:2 * P], ACT.Copy,
                                             scale=gk[:]).then_inc(s["qkT_ready"], 1)
                    if 0 <= m < N_QUADS:
                        for hh in (2, 3):
                            act.wait_ge(s["pt_done"], act.snap(b * (4 * N_QUADS) + (4 * m + hh + 1)))
                            nc.scalar.activation(probsT[:, hh, :, :].rearrange("p k q -> p (k q)"), ps[:, SC[hh], :],
                                                 ACT.Copy).then_inc(s["ptev_act"], 1)

            act.wait_ge(ld_bias, 16 * 7)
            with act.Fori(0, T // BLK) as m:
                m1 = act.snap(m + 1)
                act.wait_ge(s["gn_done"], m1)
                for c in range(KT):
                    last = nc.scalar.activation(gi_nT[:, :, B * c:B * c + B].rearrange("p t b -> p b t"),
                                                ps[:, GN, P * c:P * c + P].rearrange("p (b t) -> p b t", b=B),
                                                ACT.Identity, bias=binT[:, c:c + 1])
                last.then_inc(s["gin_ready"], 1)
                act.wait_ge(s["x1r_done"], act.snap(m + 2))
                nc.scalar.activation(x1_rows, ps[:, PH, :], ACT.Copy).then_inc(s["x1row_ready"], 1)
                for u in range(BLK):
                    t1 = act.snap(m * BLK + (u + 1))
                    act.wait_ge(s["rT_done"], t1)
                    nc.scalar.activation(b4(t_r[:]), from_block(rT_ps), ACT.Tanh, scale=0.5).then_inc(s["tr_done"], 1)
                    act.wait_ge(s["v_done"], t1)
                    nc.scalar.activation(n_new[:], v_ps, ACT.Tanh).then_inc(s["n_done"], 1)
                    act.wait_ge(s["zT_done"], act.snap(m * BLK + (u + 2)))
                    nc.scalar.activation(b4(t_z[:]), from_block(zT_ps), ACT.Tanh, scale=0.5).then_inc(s["tz_done"], 1)

        @block.vector
        def _(dve):
            prime = (("x1_ready", KT), ("qn_done", 2), ("oT_ready", 1),
                     ("gi_ready", 1), ("gin_ready", 1), ("outrow_ready", 1), ("x1r_done", 1), ("out_sent", 1))
            for name, count in prime:
                dve.sem_inc(s[name], count)
            dve.wait_ge(ld_cond, 16 * (KT + 2))
            nc.vector.tensor_scalar_add(bembT[:, 0:KT], bembT[:, 0:KT], 1.0).then_inc(s["bemb1"], 1)
            dve.wait_ge(s["emb_done"], 1)
            dve.wait_ge(s["bemb1"], 1)
            for c in range(KT):
                nc.vector.tensor_scalar(mod_all[:, :, c], ps[:, PM, B * c:B * c + B], bembT[:, c:c + 1], gnT[:, c:c + 1],
                                        ALU.add, ALU.mult)
                last = nc.vector.tensor_scalar(mod_all[:, :, KT + c], ps[:, PM, B * (KT + c):B * (KT + c) + B],
                                               bembT[:, KT + c:KT + c + 1], None, ALU.add)
            last.then_inc(s["mod_ready"], 1)
            dve.wait_ge(s["mod_ready"], 1)
            with dve.Fori(0, B) as b:
                nc.vector.tensor_copy(mod_b[:].rearrange("p (o n) -> p o n", o=1),
                                      mod_all[:, bass.ds(b, 1), :]).then_inc(s["modb_ready"], 1)
                dve.wait_ge(s["rstd_done"], dve.snap(b + 1))
                for t in range(TT):
                    nc.vector.tensor_scalar(xr[:, t, :], xb[:, t, :], rstd[:, t:t + 1], None, ALU.mult).then_inc(s["xr_ready"], 1)
                dve.wait_ge(s["modb_ready"], dve.snap(b + 1))
                for c in range(KT):
                    dve.wait_ge(s["xn_ps"], dve.snap(b * KT + (c + 1)))
                    nc.vector.tensor_scalar(xnT[:, c, :], ps[:, SC[c], :], mod_b[:, c:c + 1], mod_b[:, KT + c:KT + c + 1],
                                            ALU.mult, ALU.add).then_inc(s["xnT_ready"], 1)
                for slot in range(N_SLOTS):
                    n, m = slot, slot - LAG
                    if 0 <= m < N_QUADS:
                        for hh in range(4):
                            dve.wait_ge(s["s_done"], dve.snap(b * (4 * N_QUADS) + (4 * m + hh + 1)))
                            nc.vector.reduce_max(negmax[:, m % 2, hh:hh + 1], ps[:, SC[hh], :], AX_X,
                                                 negate=True).then_inc(s["max_done"], 1)
                    if 1 <= n <= N_TILES:
                        i = n - 1
                        dve.wait_ge(s["qkrs_done"], dve.snap(b * N_TILES + n))
                        nc.vector.tensor_tensor(
                            qn[:, i % 2, :].rearrange("p (h d) -> p h d", d=DH),
                            ps[:, PJ[i % 2], 0:2 * P].rearrange("p (h d) -> p h d", d=DH),
                            qk_rs[:, i % 2, :].unsqueeze(2).broadcast_to([P, 8, DH]), ALU.mult).then_inc(s["qn_done"], 1)
                    if 0 <= m - 1 < N_QUADS and (m - 1) % TT == TT - 1:
                        dve.wait_ge(s["pv_done"], dve.snap(b * N_QUADS + m))
                        dve.wait_ge(s["r_ready"], dve.snap(b * N_QUADS + m))
                        nc.vector.tensor_tensor(oT[:, (m - 1) // TT, :], ps[:, PO, :], rT_sb[:], ALU.mult).then_inc(s["oT_ready"], 1)
                    if 0 <= m < N_QUADS:
                        dve.wait_ge(s["exp_done"], dve.snap(b * (4 * N_QUADS) + (4 * m + 4)))
                        if m > 0:
                            dve.wait_ge(s["rtr_done"], dve.snap(b * N_QUADS + m))
                        nc.vector.reciprocal(rexp[:].rearrange("p (h d) -> p h d", d=DH),
                                             sums[:, m % 2, :].unsqueeze(2).broadcast_to([P, 4, DH])).then_inc(s["rexp_done"], 1)
                        for hh in (0, 1):
                            dve.wait_ge(s["pt_done"], dve.snap(b * (4 * N_QUADS) + (4 * m + hh + 1)))
                            nc.vector.tensor_copy(probsT[:, hh, :, :].rearrange("p k q -> p (k q)"),
                                                  ps[:, SC[hh], :]).then_inc(s["ptev_dve"], 1)
                    if n < N_TILES:
                        dve.wait_ge(s["sq_done"], dve.snap(b * N_TILES + (n + 1)))
                        nc.vector.reduce_sum(qk_ss[:, n % 2, :], sq[:, n % 2, :].rearrange("p (h d) -> p h d", d=DH),
                                             AX_X).then_inc(s["ss_done"], 1)
                dve.wait_ge(s["ox_ready"], dve.snap(b + 1))
                for c in range(KT):
                    dve.wait_ge(s["y_done"], dve.snap(b * KT + (c + 1)))
                    nc.vector.tensor_tensor(x1T[:, c, bass.ds(b, 1), :], ps[:, SC[c]:SC[c] + 1, :], xT[:, c:c + 1, :],
                                            ALU.add).then_inc(s["x1_ready"], 1)

            dve.wait_ge(s["x1_ready"], (B + 1) * KT)
            dve.wait_ge(ld_bias, 16 * 7)
            nc.vector.tensor_tensor(brz[:], brz[:], brz2[:], ALU.add).then_inc(s["brz_ready"], 1)
            nc.vector.tensor_copy(gi_rows[:, 2 * D:3 * D], bhn[:]).then_inc(s["gi_const"], 1)
            nc.vector.memset(ps[:, RQ, :], 0.0).then_inc(s["rq_read"], 1)
            nc.vector.memset(ps[:, Z, :], 0.0).then_inc(s["zT_done"], 1)
            nc.vector.memset(z_part[:], 0.0).then_inc(s["h_ready"], 1)
            dve.wait_ge(s["brz_ready"], 1)
            dve.wait_ge(ld_h0, 16 * 4 * KT)
            with dve.Fori(0, T // BLK) as m:
                m1 = dve.snap(m + 1)
                dve.wait_ge(s["gr_done"], m1)
                nc.vector.tensor_tensor(gi_rows[:, 0:D], ps[:, GR, :], brz[:, 0:D], ALU.add)
                dve.wait_ge(s["gz_done"], m1)
                nc.vector.tensor_tensor(gi_rows[:, D:2 * D], ps[:, GZ, :], brz[:, D:2 * D], ALU.add).then_inc(s["gi_ready"], 1)
                dve.wait_ge(s["gin_ready"], dve.snap(m + 2))
                for u in range(BLK):
                    t1 = dve.snap(m * BLK + (u + 1))
                    t2 = dve.snap(m * BLK + (u + 2))
                    prev, new = h_ring[:, (u - 1) % BLK, :], h_ring[:, u, :]
                    dve.wait_ge(s["rq_done"], t1)
                    nc.vector.transpose(rT_ps, ps[:, RQ, 0:P]).then_inc(s["rT_done"], 1)
                    nc.vector.transpose(qT[:], ps[:, RQ, P:2 * P]).then_inc(s["rq_read"], 1)
                    dve.wait_ge(s["rq_read"], t2)
                    nc.vector.memset(wait_mark[:], 0.0)
                    dve.wait_ge(s["tr_done"], t1)
                    nc.vector.scalar_tensor_tensor(out=b4(w_n[:]), in0=b4(t_r[:]), scalar=1.0, in1=from_block(qT[:]),
                                                   op0=ALU.add, op1=ALU.mult).then_inc(s["w_done"], 1)
                    dve.wait_ge(s["w_done"], t1)
                    nc.vector.scalar_tensor_tensor(out=v_ps, in0=w_n[:], scalar=0.5, in1=gi_nT[:, u, :],
                                                   op0=ALU.mult, op1=ALU.add).then_inc(s["v_done"], 1)
                    dve.wait_ge(s["z_done"], t1)
                    nc.vector.transpose(zT_ps, ps[:, Z, 0:P]).then_inc(s["zT_done"], 1)
                    dve.wait_ge(s["n_done"], t1)
                    nc.vector.tensor_tensor(n_plus_h[:], n_new[:], prev, ALU.add)
                    nc.vector.tensor_tensor(h_minus_n[:], prev, n_new[:], ALU.subtract).then_inc(s["sd_done"], 1)
                    dve.wait_ge(s["sd_done"], t1)
                    nc.vector.memset(wait_mark[:], 0.0)
                    dve.wait_ge(s["tz_done"], t1)
                    nc.vector.scalar_tensor_tensor(out=z_part[:], in0=h_minus_n[:], scalar=0.5, in1=t_z[:],
                                                   op0=ALU.mult, op1=ALU.mult).then_inc(s["zp_done"], 1)
                    dve.wait_ge(s["zp_done"], t1)
                    nc.vector.scalar_tensor_tensor(out=new, in0=n_plus_h[:], scalar=0.5, in1=z_part[:],
                                                   op0=ALU.mult, op1=ALU.add).then_inc(s["h_ready"], 1)
                dve.wait_ge(s["ht_done"], m1)
                dve.wait_ge(s["x1row_ready"], m1)
                dve.wait_ge(s["out_sent"], m1)
                nc.vector.tensor_tensor(out_rows.rearrange("p (j c x) -> p j c x", j=4, c=KT),
                                        ps[:, PH, :].rearrange("p (c j x) -> p j c x", c=KT, j=4),
                                        x1_rows.rearrange("p (j c x) -> p j c x", j=4, c=KT), ALU.add).then_inc(s["outrow_ready"], 1)


_INS = ["x", "cond_2048", "L0_cond_W_emb", "L0_cond_b_emb", "L0_cond_g_norm", "L0_cond_W_qkv", "L0_cond_g_q",
        "L0_cond_g_k", "L0_cond_W_out", "L1_cond_W_ih", "L1_cond_W_hh", "L1_cond_b_ih", "L1_cond_b_hh"]


def kernel(**inputs):
    import numpy as _np
    import concourse.bacc as _bacc
    from concourse import mybir as _mybir
    from concourse.bass_utils import run_bass_kernel_spmd as _run

    nc = _bacc.Bacc("TRN2", target_bir_lowering=False, num_devices=1)
    arrays, args = {}, []
    for name in _INS:
        a = _np.ascontiguousarray(inputs[name])
        arrays[f"in_{name}"] = a
        args.append(nc.dram_tensor(f"in_{name}", a.shape, _mybir.dt.from_np(a.dtype), kind="ExternalInput").ap())
    args.append(nc.dram_tensor("out_0", (B, T, D), F32, kind="ExternalOutput").ap())
    attention_gru_kernel(nc, *args)
    r = _run(nc, [arrays], core_ids=[0])
    return r.results[0]["out_0"]
```

```python
from contextlib import ExitStack

import concourse.bass as bass
from concourse import mybir

ALU = mybir.AluOpType
ACT = mybir.ActivationFunctionType
F32 = mybir.dt.float32
AX_X = mybir.AxisListType.X

P = 128
B, T, D = 4, 512, 512
HEADS = 16
DH = D // HEADS
KT = D // P
TT = T // P
G = HEADS // 4
EPS = 1e-6
BLK = P // B
QD = 32
N_TILES = G * TT
N_QUADS = G * TT
LAG = 5
N_SLOTS = N_QUADS + LAG + 1
OUT_STEP = BLK - 1


def attention_gru_kernel(nc, x, cond, W_emb, b_emb, g_norm, W_qkv, g_q, g_k, W_out,
                         W_ih, W_hh, b_ih, b_hh, out):
    with ExitStack() as ctx:
        def sb(name, shape):
            return ctx.enter_context(nc.sbuf_tensor(name, shape, F32))

        def sem(name):
            return ctx.enter_context(nc.semaphore(name))

        wqkv = sb("wqkv", [P, KT, 3 * D])
        wout = sb("wout", [P, KT, D])
        wih = sb("wih", [P, KT, 3 * D])
        whh = sb("whh", [P, KT, 3 * D])
        ident = sb("ident", [P, P])
        gq_s = sb("gq_s", [P, 1])
        gk = sb("gk", [P, 1])
        condT = sb("condT", [P, KT, B])
        bembT = sb("bembT", [P, 2 * KT])
        gnT = sb("gnT", [P, KT])
        mod_all = sb("mod_all", [P, B, 2 * KT])
        mod_b = sb("mod_b", [P, 2 * KT])
        brz = sb("brz", [P, 2 * D])
        brz2 = sb("brz2", [P, 2 * D])
        bhn = sb("bhn", [P, D])
        binT = sb("binT", [P, KT])
        half_neg = sb("half_neg", [P, 8])

        x1T = sb("x1T", [P, KT, B, T])
        wemb = x1T[:].rearrange("p k b t -> p (k b t)")[:, 0:KT * 2 * D].rearrange("p (k n) -> p k n", k=KT)

        xb = sb("xb", [P, TT, D])
        xr = sb("xr", [P, TT, D])
        xnT = sb("xnT", [P, KT, T])
        xT = sb("xT", [P, KT, T])
        ssq = sb("ssq", [P, TT])
        ms = sb("ms", [P, TT])
        rstd = sb("rstd", [P, TT])
        sq = sb("sq", [P, 2, 2 * P])
        qk_ss = sb("qk_ss", [P, 2, 8])
        qk_ms = sb("qk_ms", [P, 2, 8])
        qk_rs = sb("qk_rs", [P, 2, 8])
        qn = sb("qn", [P, 2, 2 * P])
        qkT = sb("qkT", [P, 2, 2, T])
        v_sb = sb("v_sb", [P, G, TT, P])
        probs = sb("probs", [P, 4, T])
        probsT = sb("probsT", [P, 4, TT, P])
        negmax = sb("negmax", [P, 2, 4])
        sums = sb("sums", [P, 2, 4])
        rexp = sb("rexp", [P, P])
        rT_sb = sb("rT_sb", [P, T])
        oT = sb("oT", [P, G, T])

        xr_flat = xr[:].rearrange("p a b -> p (a b)")
        xb_flat = xb[:].rearrange("p a b -> p (a b)")
        gi = xr_flat[:, 0:3 * D]
        x1_blk = xb_flat[:, 0:D].rearrange("p (c r) -> p c r", c=KT)
        out_blk = xb_flat[:, D:2 * D].rearrange("p (u r) -> p u r", r=BLK)
        out_full = xb_flat[:, 2 * D:3 * D]
        out_rows = xr_flat[:, 3 * D:4 * D]
        gi_nT = xb_flat[:, 3 * D:4 * D].rearrange("p (t u) -> p t u", t=BLK)
        state = sb("state", [P, 2, KT * B])
        qT = sb("qT", [P, P])
        gate_cols = lambda ap, g, j: ap.rearrange("p (g c j x) -> p g c j x", c=KT, j=4, x=QD)[:, g, :, j, :]
        t_r = sb("t_r", [P, 16])
        t_z = sb("t_z", [P, 16])
        n_new = sb("n_new", [P, 16])
        w_n = sb("w_n", [P, 16])
        n_plus_h = sb("n_plus_h", [P, 16])
        h_minus_n = sb("h_minus_n", [P, 16])
        z_part = sb("z_part", [P, 16])
        wait_mark = sb("wait_mark", [P, 1])

        ps = ctx.enter_context(nc.psum_tensor("ps", [P, 8, 512], F32))
        SC, PO, PJ, PM = (0, 1, 2, 3), 4, (5, 6), 7
        RQ, Z, RV, ZT, GR, GZ, GN, PH = range(8)
        rT_ps = ps[:, RV, 0:P]
        v_ps = ps[:, RV, P:P + 16]
        zT_ps = ps[:, ZT, 0:P]

        (ld_cond, ld_emb, ld_wqkv, ld_wout, ld_wih, ld_whh, ld_bias, ld_x, ld_g, st_out) = (
            sem(n) for n in ("ld_cond", "ld_emb", "ld_wqkv", "ld_wout", "ld_wih", "ld_whh", "ld_bias",
                             "ld_x", "ld_g", "st_out"))
        s = {n: sem(n) for n in (
            "ident_zero", "ident_ready", "half_ready", "emb_done", "bemb1", "mod_ready", "gq_ready",
            "ssq_done", "ms_done", "rstd_done", "modb_ready", "xr_ready", "xn_ps", "xnT_ready", "x_ps",
            "xT_ready", "out_sent", "pool_waited",
            "proj_done", "sq_done", "ss_done", "qkms_done", "qkrs_done", "qn_done", "tqk_done", "qkT_ready",
            "s_done", "max_done", "exp_done", "pt_done", "ptev_dve", "ptev_act",
            "rexp_done", "rtr_done", "r_ready", "pv_done", "oT_ready", "ox_ready", "y_done", "x1_ready",
            "brz_ready", "gi_const", "x1blk_ready", "gi_done", "gi_ready", "gin_ready", "inject_done",
            "outblk_done", "outT_done", "outrow_ready", "outfull_ready",
            "rq_done", "z_done", "rT_done", "qT_done", "zT_done",  "w_done", "v_done",
            "sd_done", "zp_done", "h_ready", "tr_done", "tz_done", "n_done")}

        b4 = lambda ap: ap.rearrange("p (c b) -> p c b", b=B)
        from_block = lambda ap: ap.rearrange("p (c r) -> p c r", r=QD)[:, :, 0:B]

        block = ctx.enter_context(nc.Block())

        @block.sync
        def _(sp):
            nat = lambda w: w.rearrange("(k p) n -> p k n", p=P)
            for k in range(KT):
                sp.dma_start(condT[:, k, :], cond[:, P * k:P * k + P].rearrange("b p -> p b"),
                             allow_slow_non_contiguous=True).then_inc(ld_cond, 16)
            sp.dma_start(bembT[:], b_emb.rearrange("(k p) -> p k", p=P), allow_slow_non_contiguous=True).then_inc(ld_cond, 16)
            sp.dma_start(gnT[:], g_norm.rearrange("(k p) -> p k", p=P), allow_slow_non_contiguous=True).then_inc(ld_cond, 16)
            sp.dma_start(xb[:], x[0].rearrange("(t p) f -> p t f", p=P)).then_inc(ld_x, 16)
            sp.dma_start(wemb, nat(W_emb)).then_inc(ld_emb, 16)
            for hh in range(4):
                sp.dma_start(gq_s[QD * hh:QD * hh + QD, :], g_q.rearrange("(d o) -> d o", o=1)).then_inc(ld_g, 16)
                sp.dma_start(gk[QD * hh:QD * hh + QD, :], g_k.rearrange("(d o) -> d o", o=1)).then_inc(ld_g, 16)
            with sp.Fori(0, B - 1) as b:
                sp.wait_ge(s["xT_ready"], sp.snap(b * KT + KT))
                sp.dma_start(xb[:], x[bass.ds(b + 1, 1), :, :].rearrange("o (t p) f -> p (o t) f", p=P)).then_inc(ld_x, 16)
            with sp.Fori(0, T // BLK) as m:
                sp.wait_ge(s["outrow_ready"], sp.snap(m + 3))
                for b in range(B):
                    sp.dma_start(out[b, bass.ds(m * BLK, BLK), :], out_rows[BLK * b:BLK * b + BLK, :]).then_inc(st_out, 16)
                sp.wait_ge(st_out, sp.snap(m * (16 * B) + 16 * B))
                sp.sem_inc(s["out_sent"], 1)
            sp.wait_ge(st_out, 16 * B * T // BLK)

        @block.gpsimd
        def _(pool):
            def await_on_pool(semaphore, value):
                pool.wait_ge(semaphore, value)
                pool.sem_inc(s["pool_waited"], 1)

            pool.dma_start(wqkv[:], W_qkv.rearrange("(k p) n -> p k n", p=P)).then_inc(ld_wqkv, 16)
            nc.gpsimd.memset(ident[:], 0.0).then_inc(s["ident_zero"], 1)
            pool.wait_ge(s["ident_zero"], 1)
            nc.gpsimd.affine_select(out=ident[:], in_=ident[:], compare_op=ALU.not_equal, fill=1.0, base=0,
                                    pattern=[[-1, P]], channel_multiplier=1).then_inc(s["ident_ready"], 1)
            nc.gpsimd.memset(half_neg[:], -0.5).then_inc(s["half_ready"], 1)
            pool.dma_start(wout[:], W_out.rearrange("(k p) n -> p k n", p=P)).then_inc(ld_wout, 16)
            pool.dma_start(wih[:], W_ih.rearrange("(k p) n -> p k n", p=P)).then_inc(ld_wih, 16)
            pool.dma_start(whh[:], W_hh.rearrange("(k p) n -> p k n", p=P)).then_inc(ld_whh, 16)
            pool.dma_start(binT[:], b_ih[2 * D:3 * D].rearrange("(k p) -> p k", p=P),
                           allow_slow_non_contiguous=True).then_inc(ld_bias, 16)
            pool.dma_start(brz[:], b_ih[0:2 * D].partition_broadcast(P)).then_inc(ld_bias, 16)
            pool.dma_start(brz2[:], b_hh[0:2 * D].partition_broadcast(P)).then_inc(ld_bias, 16)
            pool.dma_start(bhn[:], b_hh[2 * D:3 * D].partition_broadcast(P)).then_inc(ld_bias, 16)

            pool.wait_ge(s["half_ready"], 1)
            with pool.Fori(0, B) as b:
                b1 = pool.snap(b + 1)
                await_on_pool(s["ssq_done"], b1)
                nc.gpsimd.tensor_scalar(ms[:], ssq[:], 1.0 / D, EPS, ALU.mult, ALU.add).then_inc(s["ms_done"], 1)
                await_on_pool(s["ms_done"], b1)
                nc.gpsimd.tensor_tensor(rstd[:], ms[:], half_neg[:, 0:TT], ALU.pow).then_inc(s["rstd_done"], 1)
                for n in range(N_TILES):
                    n1 = pool.snap(b * N_TILES + (n + 1))
                    await_on_pool(s["ss_done"], n1)
                    nc.gpsimd.tensor_scalar(qk_ms[:, n % 2], qk_ss[:, n % 2], 1.0 / DH, EPS, ALU.mult, ALU.add).then_inc(s["qkms_done"], 1)
                    await_on_pool(s["qkms_done"], n1)
                    nc.gpsimd.tensor_tensor(qk_rs[:, n % 2], qk_ms[:, n % 2], half_neg[:], ALU.pow).then_inc(s["qkrs_done"], 1)
                await_on_pool(s["oT_ready"], pool.snap(b * G + (G + 1)))
                await_on_pool(s["xT_ready"], pool.snap(b * KT + KT))
                nc.gpsimd.tensor_tensor(xT[:].rearrange("p k t -> p (k t)"), xT[:].rearrange("p k t -> p (k t)"),
                                        oT[:].rearrange("p k t -> p (k t)"), ALU.add).then_inc(s["ox_ready"], 1)

            def copy_x1(first):
                nc.gpsimd.tensor_copy(x1_blk.rearrange("p c (b t) -> p (c b) t", b=B),
                                      x1T[:].rearrange("p c b t -> p (c b) t")[:, :, bass.ds(first, BLK)]
                                      ).then_inc(s["x1blk_ready"], 1)

            await_on_pool(s["x1_ready"], (B + 1) * KT)
            copy_x1(0)
            await_on_pool(s["gi_done"], 1)
            copy_x1(BLK)
            with pool.Fori(0, T // BLK) as m:
                await_on_pool(s["gi_done"], pool.snap(m + 2))
                copy_x1((m + 2) % (T // BLK) * BLK)
                await_on_pool(s["outblk_done"], pool.snap(m * BLK + BLK))
                await_on_pool(s["outT_done"], pool.snap(m + 1))
                nc.gpsimd.tensor_copy(out_full, out_blk.rearrange("p u r -> p (u r)")).then_inc(s["outfull_ready"], 1)

        @block.tensor
        def _(pe):
            def transpose(dst, src):
                return nc.tensor.transpose(dst, src, ident[:])

            pe.wait_ge(s["ident_ready"], 1)
            pe.wait_ge(ld_cond, 16 * (KT + 2))
            pe.wait_ge(ld_emb, 16)
            for c in range(2 * KT):
                for k in range(KT):
                    last = nc.tensor.matmul(ps[:, PM, B * c:B * c + B], wemb[:, k, P * c:P * c + P], condT[:, k, :],
                                            start=(k == 0), stop=(k == KT - 1))
            last.then_inc(s["emb_done"], 1)
            pe.wait_ge(s["mod_ready"], 1)

            with pe.Fori(0, B) as b:
                for c in range(KT):
                    pe.wait_ge(s["x1_ready"], pe.snap(b * KT + (c + 1)))
                    for t in range(TT):
                        if c == 0:
                            pe.wait_ge(s["xr_ready"], pe.snap(b * TT + (t + 1)))
                        last = transpose(ps[:, SC[c], P * t:P * t + P], xr[:, t, P * c:P * c + P])
                    last.then_inc(s["xn_ps"], 1)
                for c in range(KT):
                    pe.wait_ge(s["xnT_ready"], pe.snap(b * KT + (c + 1)))
                    for t in range(TT):
                        last = transpose(ps[:, SC[c], P * t:P * t + P], xb[:, t, P * c:P * c + P])
                    last.then_inc(s["x_ps"], 1)
                pe.wait_ge(ld_wqkv, 16)
                for slot in range(N_SLOTS):
                    n, m = slot, slot - LAG
                    if 0 <= m < N_QUADS:
                        g, q = divmod(m, TT)
                        if q == 0:
                            pe.wait_ge(s["qkT_ready"], pe.snap(b * N_TILES + (TT * g + TT)))
                        for hh in range(4):
                            if m == 0:
                                pe.wait_ge(s["xT_ready"], pe.snap(b * KT + (hh + 1)))
                            elif hh < 2:
                                pe.wait_ge(s["ptev_dve"], pe.snap(b * (2 * N_QUADS) + (2 * m - 1 + hh)))
                            else:
                                pe.wait_ge(s["ptev_act"], pe.snap(b * (2 * N_QUADS) + (2 * m - 3 + hh)))
                            r = slice(QD * hh, QD * hh + QD)
                            nc.tensor.matmul(ps[:, SC[hh], :], qkT[r, g % 2, 0, P * q:P * q + P], qkT[r, g % 2, 1, :],
                                             start=True, stop=True, tile_position=(QD * hh, 0)).then_inc(s["s_done"], 1)
                    if 0 <= m - 1 < N_QUADS:
                        g, q = divmod(m - 1, TT)
                        u1 = b * N_QUADS + m
                        if q == 0:
                            pe.wait_ge(s["oT_ready"], pe.snap(b * G + (g + 1)))
                        pe.wait_ge(s["rexp_done"], pe.snap(u1))
                        pe.wait_ge(s["qkT_ready"], pe.snap(b * N_TILES + min(slot - 1, N_TILES)))
                        transpose(ps[:, PM, 0:P], rexp[:]).then_inc(s["rtr_done"], 1)
                        pe.wait_ge(s["ptev_dve"], pe.snap(b * (2 * N_QUADS) + 2 * m))
                        pe.wait_ge(s["ptev_act"], pe.snap(b * (2 * N_QUADS) + 2 * m))
                        for kc in range(TT):
                            for hh in range(4):
                                last = nc.tensor.matmul(
                                    ps[QD * hh:QD * hh + QD, PO, P * q:P * q + P],
                                    v_sb[:, g, kc, QD * hh:QD * hh + QD], probsT[:, hh, kc, :],
                                    start=(kc == 0), stop=(kc == TT - 1), tile_position=(0, QD * hh))
                        last.then_inc(s["pv_done"], 1)
                    if n < N_TILES:
                        g, t = divmod(n, TT)
                        if n == 0:
                            pe.wait_ge(s["xnT_ready"], pe.snap(b * KT + KT))
                        pe.wait_ge(s["qn_done"], pe.snap(b * N_TILES + (n + 1)))
                        for k in range(KT):
                            last = nc.tensor.matmul(ps[:, PJ[n % 2], 0:3 * P], xnT[:, k, P * t:P * t + P],
                                                    wqkv[:, k, :].rearrange("p (a g n) -> p a g n", a=3, g=G)[:, :, g, :],
                                                    start=(k == 0), stop=(k == KT - 1))
                        last.then_inc(s["proj_done"], 1)
                    if 1 <= n <= N_TILES:
                        pe.wait_ge(s["qn_done"], pe.snap(b * N_TILES + (n + 2)))
                        if n >= 2:
                            pe.wait_ge(s["qkT_ready"], pe.snap(b * N_TILES + (n - 1)))
                        if 0 <= m - 1:
                            pe.wait_ge(s["r_ready"], pe.snap(b * N_QUADS + m))
                        transpose(ps[:, PM, 0:P], qn[:, (n - 1) % 2, 0:P])
                        transpose(ps[:, PM, P:2 * P], qn[:, (n - 1) % 2, P:2 * P]).then_inc(s["tqk_done"], 1)
                    if 0 <= m < N_QUADS:
                        for hh in range(4):
                            pe.wait_ge(s["exp_done"], pe.snap(b * (4 * N_QUADS) + (4 * m + hh + 1)))
                            for kc in range(TT):
                                last = transpose(ps[:, SC[hh], P * kc:P * kc + P], probs[:, hh, P * kc:P * kc + P])
                            last.then_inc(s["pt_done"], 1)
                pe.wait_ge(ld_wout, 16)
                pe.wait_ge(s["oT_ready"], pe.snap(b * G + (G + 1)))
                for c in range(KT):
                    for k in range(KT):
                        last = nc.tensor.matmul(ps[:, SC[c], :], wout[:, k, P * c:P * c + P], oT[:, k, :],
                                                start=(k == 0), stop=(k == KT - 1))
                    last.then_inc(s["y_done"], 1)

            pe.wait_ge(ld_wih, 16)
            pe.wait_ge(ld_whh, 16)

            GI_PIECES = [(gate, c, k) for gate in range(3) for c in range(KT) for k in range(KT)]

            def gi_pieces(pieces):
                for gate, c, k in pieces:
                    cols = slice(D * gate + P * c, D * gate + P * c + P)
                    lhsT, rhs = (wih[:, k, cols], x1_blk[:, k, :]) if gate == 2 else (x1_blk[:, k, :], wih[:, k, cols])
                    last = nc.tensor.matmul(ps[:, (GR, GZ, GN)[gate], P * c:P * c + P], lhsT, rhs,
                                            start=(k == 0), stop=(k == KT - 1))
                return last

            def pieces_of(u):
                return GI_PIECES[len(GI_PIECES) * u // (BLK - 1):len(GI_PIECES) * (u + 1) // (BLK - 1)]

            def inject(bank, width, gates, u):
                for j in range(4):
                    last = nc.tensor.matmul(ps[QD * j:QD * j + B, bank, 0:width], ident[:, u::BLK], gate_cols(gi, gates, j),
                                            start=True, stop=False, tile_position=(0, QD * j))
                return last

            def add_hidden_side(bank, width, gates, prev):
                for k in range(KT):
                    for j in range(4):
                        last = nc.tensor.matmul(ps[QD * j:QD * j + B, bank, 0:width], prev[:, B * k:B * k + B],
                                                gate_cols(whh[:, k, :], gates, j), start=False, stop=(k == KT - 1),
                                                tile_position=(0, QD * j))
                return last

            R_AND_N, Z_ONLY = slice(0, 3, 2), 1

            def output_rows():
                for c in range(KT):
                    last = transpose(ps[:, PH, P * c:P * c + P], out_full[:, P * c:P * c + P])
                return last

            pe.wait_ge(s["x1blk_ready"], 1)
            gi_pieces(GI_PIECES).then_inc(s["gi_done"], 1)
            pe.wait_ge(s["gi_ready"], 1)
            pe.wait_ge(s["gi_const"], 1)
            pe.wait_ge(s["qT_done"], 1)
            inject(RQ, 2 * P, R_AND_N, 0)
            pe.wait_ge(s["zT_done"], 1)
            inject(Z, P, Z_ONLY, 0).then_inc(s["inject_done"], 1)
            with pe.Fori(0, T // BLK) as m:
                for u in range(BLK):
                    t1 = pe.snap(m * BLK + (u + 1))
                    t2 = pe.snap(m * BLK + (u + 2))
                    pe.wait_ge(s["h_ready"], t1)
                    add_hidden_side(RQ, 2 * P, R_AND_N, state[:, (u - 1) % 2, :]).then_inc(s["rq_done"], 1)
                    add_hidden_side(Z, P, Z_ONLY, state[:, (u - 1) % 2, :]).then_inc(s["z_done"], 1)
                    if u == BLK - 1:
                        pe.wait_ge(s["gi_ready"], pe.snap(m + 2))
                    pe.wait_ge(s["qT_done"], t2)
                    inject(RQ, 2 * P, R_AND_N, (u + 1) % BLK)
                    if u == 0:
                        pe.wait_ge(s["x1blk_ready"], pe.snap(m + 2))
                        pe.wait_ge(s["gin_ready"], pe.snap(m + 1))
                    if u < BLK - 1:
                        last = gi_pieces(pieces_of(u))
                    if u == BLK - 2:
                        last.then_inc(s["gi_done"], 1)
                    pe.wait_ge(s["zT_done"], t2)
                    inject(Z, P, Z_ONLY, (u + 1) % BLK).then_inc(s["inject_done"], 1)
                    if u == OUT_STEP:
                        pe.wait_ge(s["outfull_ready"], pe.snap(m + 1))
                        pe.wait_ge(s["outrow_ready"], pe.snap(m + 1))
                        output_rows().then_inc(s["outT_done"], 1)
            pe.wait_ge(s["outfull_ready"], T // BLK + 1)
            pe.wait_ge(s["outrow_ready"], T // BLK + 1)
            output_rows().then_inc(s["outT_done"], 1)

        @block.scalar
        def _(act):
            act.wait_ge(ld_g, 128)
            nc.scalar.mul(gq_s[:], gq_s[:], DH ** -0.5).then_inc(s["gq_ready"], 1)
            with act.Fori(0, B) as b:
                b1 = act.snap(b + 1)
                act.wait_ge(ld_x, act.snap(b * 16 + 16))
                for t in range(TT):
                    last = nc.scalar.activation(probs[:, t, :], xb[:, t, :], ACT.Square, accum_out=ssq[:, t:t + 1])
                last.then_inc(s["ssq_done"], 1)
                for c in range(KT):
                    act.wait_ge(s["x_ps"], act.snap(b * KT + (c + 1)))
                    if c == 0:
                        act.wait_ge(s["x1_ready"], act.snap(b * KT + KT))
                    nc.scalar.activation(xT[:, c, :], ps[:, SC[c], :], ACT.Copy).then_inc(s["xT_ready"], 1)
                act.wait_ge(s["gq_ready"], 1)
                for slot in range(N_SLOTS):
                    n, m = slot, slot - LAG
                    if 0 <= m - 1 < N_QUADS:
                        g, q = divmod(m - 1, TT)
                        act.wait_ge(s["rtr_done"], act.snap(b * N_QUADS + m))
                        nc.scalar.activation(rT_sb[:, P * q:P * q + P], ps[:, PM, 0:P], ACT.Copy).then_inc(s["r_ready"], 1)
                    if 0 <= m < N_QUADS:
                        for hh in range(4):
                            act.wait_ge(s["max_done"], act.snap(b * (4 * N_QUADS) + (4 * m + hh + 1)))
                            nc.scalar.activation(probs[:, hh, :], ps[:, SC[hh], :], ACT.Exp,
                                                 bias=negmax[:, m % 2, hh:hh + 1],
                                                 accum_out=sums[:, m % 2, hh:hh + 1]).then_inc(s["exp_done"], 1)
                    if n < N_TILES:
                        g, t = divmod(n, TT)
                        act.wait_ge(s["proj_done"], act.snap(b * N_TILES + (n + 1)))
                        nc.scalar.activation(v_sb[:, g, t, :], ps[:, PJ[n % 2], 2 * P:3 * P], ACT.Copy)
                        nc.scalar.activation(sq[:, n % 2, :], ps[:, PJ[n % 2], 0:2 * P], ACT.Square).then_inc(s["sq_done"], 1)
                    if 1 <= n <= N_TILES:
                        g, t = divmod(n - 1, TT)
                        act.wait_ge(s["tqk_done"], act.snap(b * N_TILES + n))
                        nc.scalar.activation(qkT[:, g % 2, 0, P * t:P * t + P], ps[:, PM, 0:P], ACT.Copy, scale=gq_s[:])
                        nc.scalar.activation(qkT[:, g % 2, 1, P * t:P * t + P], ps[:, PM, P:2 * P], ACT.Copy,
                                             scale=gk[:]).then_inc(s["qkT_ready"], 1)
                    if 0 <= m < N_QUADS:
                        for hh in (2, 3):
                            act.wait_ge(s["pt_done"], act.snap(b * (4 * N_QUADS) + (4 * m + hh + 1)))
                            nc.scalar.activation(probsT[:, hh, :, :].rearrange("p k q -> p (k q)"), ps[:, SC[hh], :],
                                                 ACT.Copy).then_inc(s["ptev_act"], 1)

            act.wait_ge(ld_bias, 16 * 4)
            def evacuate_gi_n():
                for c in range(KT):
                    last = nc.scalar.activation(gi_nT[:, :, B * c:B * c + B].rearrange("p t b -> p b t"),
                                                ps[:, GN, P * c:P * c + P].rearrange("p (b t) -> p b t", b=B),
                                                ACT.Identity, bias=binT[:, c:c + 1])
                return last

            def evacuate_rows():
                return nc.scalar.activation(out_rows, ps[:, PH, :], ACT.Copy)

            act.wait_ge(s["gi_done"], 1)
            evacuate_gi_n().then_inc(s["gin_ready"], 1)
            with act.Fori(0, T // BLK) as m:
                for u in range(BLK):
                    t1 = act.snap(m * BLK + (u + 1))
                    t2 = act.snap(m * BLK + (u + 2))
                    act.wait_ge(s["rT_done"], t1)
                    nc.scalar.activation(b4(t_r[:]), from_block(rT_ps), ACT.Tanh, scale=0.5).then_inc(s["tr_done"], 1)
                    act.wait_ge(s["v_done"], t1)
                    nc.scalar.activation(n_new[:], v_ps, ACT.Tanh).then_inc(s["n_done"], 1)
                    act.wait_ge(s["zT_done"], t2)
                    nc.scalar.activation(b4(t_z[:]), from_block(zT_ps), ACT.Tanh, scale=0.5).then_inc(s["tz_done"], 1)
                act.wait_ge(s["gi_done"], act.snap(m + 2))
                evacuate_gi_n().then_inc(s["gin_ready"], 1)
                act.wait_ge(s["outT_done"], act.snap(m + 1))
                act.wait_ge(s["out_sent"], act.snap(m + 1))
                evacuate_rows().then_inc(s["outrow_ready"], 1)
            act.wait_ge(s["outT_done"], T // BLK + 1)
            act.wait_ge(s["out_sent"], T // BLK + 1)
            evacuate_rows().then_inc(s["outrow_ready"], 1)

        @block.vector
        def _(dve):
            prime = (("x1_ready", KT), ("qn_done", 2), ("oT_ready", 1), ("outrow_ready", 1), ("out_sent", 2))
            for name, count in prime:
                dve.sem_inc(s[name], count)
            dve.wait_ge(ld_cond, 16 * (KT + 2))
            nc.vector.tensor_scalar_add(bembT[:, 0:KT], bembT[:, 0:KT], 1.0).then_inc(s["bemb1"], 1)
            dve.wait_ge(s["emb_done"], 1)
            dve.wait_ge(s["bemb1"], 1)
            for c in range(KT):
                nc.vector.tensor_scalar(mod_all[:, :, c], ps[:, PM, B * c:B * c + B], bembT[:, c:c + 1], gnT[:, c:c + 1],
                                        ALU.add, ALU.mult)
                last = nc.vector.tensor_scalar(mod_all[:, :, KT + c], ps[:, PM, B * (KT + c):B * (KT + c) + B],
                                               bembT[:, KT + c:KT + c + 1], None, ALU.add)
            last.then_inc(s["mod_ready"], 1)
            dve.wait_ge(s["mod_ready"], 1)
            with dve.Fori(0, B) as b:
                nc.vector.tensor_copy(mod_b[:].rearrange("p (o n) -> p o n", o=1),
                                      mod_all[:, bass.ds(b, 1), :]).then_inc(s["modb_ready"], 1)
                dve.wait_ge(s["rstd_done"], dve.snap(b + 1))
                for t in range(TT):
                    nc.vector.tensor_scalar(xr[:, t, :], xb[:, t, :], rstd[:, t:t + 1], None, ALU.mult).then_inc(s["xr_ready"], 1)
                dve.wait_ge(s["modb_ready"], dve.snap(b + 1))
                for c in range(KT):
                    dve.wait_ge(s["xn_ps"], dve.snap(b * KT + (c + 1)))
                    nc.vector.tensor_scalar(xnT[:, c, :], ps[:, SC[c], :], mod_b[:, c:c + 1], mod_b[:, KT + c:KT + c + 1],
                                            ALU.mult, ALU.add).then_inc(s["xnT_ready"], 1)
                for slot in range(N_SLOTS):
                    n, m = slot, slot - LAG
                    if 0 <= m < N_QUADS:
                        for hh in range(4):
                            dve.wait_ge(s["s_done"], dve.snap(b * (4 * N_QUADS) + (4 * m + hh + 1)))
                            nc.vector.reduce_max(negmax[:, m % 2, hh:hh + 1], ps[:, SC[hh], :], AX_X,
                                                 negate=True).then_inc(s["max_done"], 1)
                    if 1 <= n <= N_TILES:
                        i = n - 1
                        dve.wait_ge(s["qkrs_done"], dve.snap(b * N_TILES + n))
                        nc.vector.tensor_tensor(
                            qn[:, i % 2, :].rearrange("p (h d) -> p h d", d=DH),
                            ps[:, PJ[i % 2], 0:2 * P].rearrange("p (h d) -> p h d", d=DH),
                            qk_rs[:, i % 2, :].unsqueeze(2).broadcast_to([P, 8, DH]), ALU.mult).then_inc(s["qn_done"], 1)
                    if 0 <= m - 1 < N_QUADS and (m - 1) % TT == TT - 1:
                        dve.wait_ge(s["pv_done"], dve.snap(b * N_QUADS + m))
                        dve.wait_ge(s["r_ready"], dve.snap(b * N_QUADS + m))
                        nc.vector.tensor_tensor(oT[:, (m - 1) // TT, :], ps[:, PO, :], rT_sb[:], ALU.mult).then_inc(s["oT_ready"], 1)
                    if 0 <= m < N_QUADS:
                        dve.wait_ge(s["exp_done"], dve.snap(b * (4 * N_QUADS) + (4 * m + 4)))
                        if m > 0:
                            dve.wait_ge(s["rtr_done"], dve.snap(b * N_QUADS + m))
                        nc.vector.reciprocal(rexp[:].rearrange("p (h d) -> p h d", d=DH),
                                             sums[:, m % 2, :].unsqueeze(2).broadcast_to([P, 4, DH])).then_inc(s["rexp_done"], 1)
                        for hh in (0, 1):
                            dve.wait_ge(s["pt_done"], dve.snap(b * (4 * N_QUADS) + (4 * m + hh + 1)))
                            nc.vector.tensor_copy(probsT[:, hh, :, :].rearrange("p k q -> p (k q)"),
                                                  ps[:, SC[hh], :]).then_inc(s["ptev_dve"], 1)
                    if n < N_TILES:
                        dve.wait_ge(s["sq_done"], dve.snap(b * N_TILES + (n + 1)))
                        nc.vector.reduce_sum(qk_ss[:, n % 2, :], sq[:, n % 2, :].rearrange("p (h d) -> p h d", d=DH),
                                             AX_X).then_inc(s["ss_done"], 1)
                dve.wait_ge(s["ox_ready"], dve.snap(b + 1))
                for c in range(KT):
                    dve.wait_ge(s["y_done"], dve.snap(b * KT + (c + 1)))
                    nc.vector.tensor_tensor(x1T[:, c, bass.ds(b, 1), :], ps[:, SC[c]:SC[c] + 1, :], xT[:, c:c + 1, :],
                                            ALU.add).then_inc(s["x1_ready"], 1)

            dve.wait_ge(s["x1_ready"], (B + 1) * KT)
            dve.wait_ge(ld_bias, 16 * 4)
            nc.vector.tensor_tensor(brz[:], brz[:], brz2[:], ALU.add).then_inc(s["brz_ready"], 1)
            nc.vector.tensor_copy(gi[:, 2 * D:3 * D], bhn[:]).then_inc(s["gi_const"], 1)
            nc.vector.memset(ps[:, RQ, :], 0.0).then_inc(s["qT_done"], 1)
            nc.vector.memset(out_full, 0.0).then_inc(s["outfull_ready"], 1)
            nc.vector.memset(ps[:, Z, :], 0.0).then_inc(s["zT_done"], 1)
            nc.vector.tensor_copy(state[:, 1, :], condT[:].rearrange("p k b -> p (k b)")).then_inc(s["h_ready"], 1)
            dve.wait_ge(s["brz_ready"], 1)

            def evacuate_gi_rz():
                nc.vector.tensor_tensor(gi[:, 0:D], ps[:, GR, :], brz[:, 0:D], ALU.add)
                return nc.vector.tensor_tensor(gi[:, D:2 * D], ps[:, GZ, :], brz[:, D:2 * D], ALU.add)

            dve.wait_ge(s["gi_done"], 1)
            evacuate_gi_rz().then_inc(s["gi_ready"], 1)
            dve.wait_ge(s["h_ready"], 1)
            with dve.Fori(0, T // BLK) as m:
                for u in range(BLK):
                    t1 = dve.snap(m * BLK + (u + 1))
                    t2 = dve.snap(m * BLK + (u + 2))
                    prev, new = state[:, (u - 1) % 2, :], state[:, u % 2, :]
                    if u == BLK - 1:
                        dve.wait_ge(s["inject_done"], t1)
                        dve.wait_ge(s["gi_done"], dve.snap(m + 2))
                        evacuate_gi_rz().then_inc(s["gi_ready"], 1)
                    dve.wait_ge(s["rq_done"], t1)
                    nc.vector.transpose(rT_ps, ps[:, RQ, 0:P]).then_inc(s["rT_done"], 1)
                    nc.vector.transpose(qT[:], ps[:, RQ, P:2 * P]).then_inc(s["qT_done"], 1)
                    if u == 0:
                        dve.wait_ge(s["gin_ready"], dve.snap(m + 1))
                    dve.wait_ge(s["tr_done"], t1)
                    dve.wait_ge(s["qT_done"], t2)
                    nc.vector.scalar_tensor_tensor(out=b4(w_n[:]), in0=b4(t_r[:]), scalar=1.0, in1=from_block(qT[:]),
                                                   op0=ALU.add, op1=ALU.mult).then_inc(s["w_done"], 1)
                    dve.wait_ge(s["w_done"], t1)
                    nc.vector.scalar_tensor_tensor(out=v_ps, in0=w_n[:], scalar=0.5, in1=gi_nT[:, u, :],
                                                   op0=ALU.mult, op1=ALU.add).then_inc(s["v_done"], 1)
                    dve.wait_ge(s["z_done"], t1)
                    nc.vector.transpose(zT_ps, ps[:, Z, 0:P]).then_inc(s["zT_done"], 1)
                    dve.wait_ge(s["n_done"], t1)
                    nc.vector.tensor_tensor(h_minus_n[:], prev, n_new[:], ALU.subtract)
                    nc.vector.tensor_tensor(n_plus_h[:], n_new[:], prev, ALU.add).then_inc(s["sd_done"], 1)
                    dve.wait_ge(s["sd_done"], t1)
                    nc.vector.memset(wait_mark[:], 0.0)
                    dve.wait_ge(s["tz_done"], t1)
                    nc.vector.scalar_tensor_tensor(out=z_part[:], in0=h_minus_n[:], scalar=0.5, in1=t_z[:],
                                                   op0=ALU.mult, op1=ALU.mult).then_inc(s["zp_done"], 1)
                    dve.wait_ge(s["zp_done"], t1)
                    nc.vector.scalar_tensor_tensor(out=new, in0=n_plus_h[:], scalar=0.5, in1=z_part[:],
                                                   op0=ALU.mult, op1=ALU.add).then_inc(s["h_ready"], 1)
                    dve.wait_ge(s["h_ready"], t2)
                    if u == 0:
                        dve.wait_ge(s["outfull_ready"], dve.snap(m + 1))
                    nc.vector.tensor_tensor(out_blk[:, :, u:u + 1], new.unsqueeze(2),
                                            x1T[:].rearrange("p c b t -> p (c b) t")[:, :, bass.ds(m * BLK + u, 1)],
                                            ALU.add).then_inc(s["outblk_done"], 1)


_INS = ["x", "cond_2048", "L0_cond_W_emb", "L0_cond_b_emb", "L0_cond_g_norm", "L0_cond_W_qkv", "L0_cond_g_q",
        "L0_cond_g_k", "L0_cond_W_out", "L1_cond_W_ih", "L1_cond_W_hh", "L1_cond_b_ih", "L1_cond_b_hh"]


def kernel(**inputs):
    import numpy as _np
    import concourse.bacc as _bacc
    from concourse import mybir as _mybir
    from concourse.bass_utils import run_bass_kernel_spmd as _run

    nc = _bacc.Bacc("TRN2", target_bir_lowering=False, num_devices=1)
    arrays, args = {}, []
    for name in _INS:
        a = _np.ascontiguousarray(inputs[name])
        arrays[f"in_{name}"] = a
        args.append(nc.dram_tensor(f"in_{name}", a.shape, _mybir.dt.from_np(a.dtype), kind="ExternalInput").ap())
    args.append(nc.dram_tensor("out_0", (B, T, D), F32, kind="ExternalOutput").ap())
    attention_gru_kernel(nc, *args)
    r = _run(nc, [arrays], core_ids=[0])
    return r.results[0]["out_0"]
```

```python
from contextlib import ExitStack

import concourse.bass as bass
from concourse import mybir

ALU = mybir.AluOpType
ACT = mybir.ActivationFunctionType
F32 = mybir.dt.float32
F32R = mybir.dt.float32r
AX_X = mybir.AxisListType.X

P = 128
B, T, D = 4, 512, 512
HEADS = 16
DH = D // HEADS
KT = D // P
TT = T // P
G = HEADS // 4
EPS = 1e-6
BLK = P // B
QD = 32
N_TILES = G * TT
N_QUADS = G * TT
LAG = 6
N_SLOTS = N_QUADS + LAG + 1
OUT_STEP = BLK - 1


def attention_gru_kernel(nc, x, cond, W_emb, b_emb, g_norm, W_qkv, g_q, g_k, W_out,
                         W_ih, W_hh, b_ih, b_hh, out):
    with ExitStack() as ctx:
        def sb(name, shape):
            return ctx.enter_context(nc.sbuf_tensor(name, shape, F32))

        def sem(name):
            return ctx.enter_context(nc.semaphore(name))

        wqkv = sb("wqkv", [P, KT, 3 * D])
        whh = wqkv
        wout = sb("wout", [P, KT, D])
        wih = sb("wih", [P, KT, 3 * D])
        stacks = ctx.enter_context(nc.sbuf_tensor("stacks", [P, 2, 2, 4, T], F32R))
        ident = sb("ident", [P, P])
        ident_r = ctx.enter_context(nc.sbuf_tensor("ident_r", [P, P], F32R))
        g_row = sb("g_row", [P, 2, 4, DH])
        condT = sb("condT", [P, KT, B])
        bembT = sb("bembT", [P, 2 * KT])
        gnT = sb("gnT", [P, KT])
        mod_all = sb("mod_all", [P, B, 2 * KT])
        mod_b = sb("mod_b", [P, 2 * KT])
        brz = sb("brz", [P, 2 * D])
        binT = sb("binT", [P, KT])

        x1T = sb("x1T", [P, KT, B, T])
        wemb = x1T[:].rearrange("p k b t -> p (k b t)")[:, 0:KT * 2 * D].rearrange("p (k n) -> p k n", k=KT)

        xb = sb("xb", [P, TT, D])
        xr = sb("xr", [P, TT, D])
        xnT = sb("xnT", [P, KT, T])
        xT = sb("xT", [P, KT, T])
        ssq = sb("ssq", [P, TT])
        ms = sb("ms", [P, TT])
        half_neg = sb("half_neg", [P, 8])
        rstd = sb("rstd", [P, TT])
        sq = sb("sq", [P, 2, 2 * P])
        embT = sq[:, 0, :]
        qk_ss = sb("qk_ss", [P, 2, 8])
        qk_ms = sb("qk_ms", [P, 2, 8])
        qk_rs = sb("qk_rs", [P, 2, 8])
        qn = sb("qn", [P, 2, 2 * P])
        norm_qk = sb("norm_qk", [P, 2, 2 * P])
        split = ctx.enter_context(nc.sbuf_tensor("split", [P, 2, 4, 4, DH], F32R))
        v_sb = sb("v_sb", [P, G, TT, P])
        probs = sb("probs", [P, 4, T])
        probsT = sb("probsT", [P, 4, TT, P])
        negmax = sb("negmax", [P, 2, 4])
        sums = sb("sums", [P, 2, 4])
        recip = sb("recip", [P, 4])
        rexp = sb("rexp", [P, P])
        rT_sb = sb("rT_sb", [P, 2, T])
        oT = sb("oT", [P, G, T])

        xr_flat = xr[:].rearrange("p a b -> p (a b)")
        xb_flat = xb[:].rearrange("p a b -> p (a b)")
        gi = xr_flat[:, 0:3 * D]
        brz2 = gi[:, 0:2 * D]
        x1_blk = xb_flat[:, 0:D].rearrange("p (c r) -> p c r", c=KT)
        out_blk = xb_flat[:, D:2 * D].rearrange("p (u r) -> p u r", r=BLK)
        out_full = xb_flat[:, 2 * D:3 * D]
        out_rows = xr_flat[:, 3 * D:4 * D]
        gi_nT = xb_flat[:, 3 * D:4 * D].rearrange("p (t u) -> p t u", t=BLK)
        state = sb("state", [P, 2, KT * B])
        qT = sb("qT", [P, P])
        gate_cols = lambda ap, g, j: ap.rearrange("p (g c j x) -> p g c j x", c=KT, j=4, x=QD)[:, g, :, j, :]
        t_r = sb("t_r", [P, 16])
        t_z = sb("t_z", [P, 16])
        n_new = sb("n_new", [P, 16])
        w_n = sb("w_n", [P, 16])
        n_plus_h = sb("n_plus_h", [P, 16])
        h_minus_n = sb("h_minus_n", [P, 16])
        z_part = sb("z_part", [P, 16])
        wait_mark = sb("wait_mark", [P, 1])

        ps = ctx.enter_context(nc.psum_tensor("ps", [P, 8, 512], F32))
        SC, PO, PJ, PM = (0, 1, 2, 3), 4, (5, 6), 7
        pj = lambda n: SC[n] if n < 4 else PJ[n % 2]
        X_BANKS = (PO, PJ[0], PJ[1], PM)
        RQ, Z, RV, ZT, GR, GZ, GN, PH = range(8)
        rT_ps = ps[:, RV, 0:P]
        v_ps = ps[:, RV, P:P + 16]
        zT_ps = ps[:, ZT, 0:P]

        (ld_cond, ld_emb, ld_wqkv, ld_wout, ld_wih, ld_whh, ld_bias, ld_bias2, ld_x, ld_g, st_out) = (
            sem(n) for n in ("ld_cond", "ld_emb", "ld_wqkv", "ld_wout", "ld_wih", "ld_whh", "ld_bias", "ld_bias2",
                             "ld_x", "ld_g", "st_out"))
        s = {n: sem(n) for n in (
            "ident_zero", "ident_ready", "identr_ready", "emb_done", "bemb1", "gn_ready", "pm_zero", "embT_done", "mod_ready", "gk_ready",
            "ssq_done", "rstd_done", "modb_ready", "xr_ready", "xn_ps", "xnT_dve", "xnT_act", "x_ps",
            "xT_ready", "out_sent", "pool_waited",
            "proj_done", "sq_done", "ss_done", "recip_done", "half_ready", "norm_done", "high_done", "split_ready", "ms_done", "qkms_done", "qkrs_done", "qn_done", "tq_done", "tk_done", "qT_ready", "kT_ready",
            "s_done", "max_done", "exp_done", "pt_done", "ptev_dve", "ptev_act",
            "rexp_done", "rtr_done", "r_ready", "pv_done", "oT_ready", "ox_ready", "y_done", "x1_ready",
            "brz_ready",  "x1blk_ready", "gi_done", "gi_ready", "gin_ready", "inject_done",
            "outblk_done", "outT_done", "outrow_ready", "outfull_ready",
            "rq_done", "z_done", "rT_done", "qT_done", "zT_done",  "w_done", "v_done",
            "sd_done", "zp_done", "h_ready", "tr_done", "tz_done", "n_done")}

        b4 = lambda ap: ap.rearrange("p (c b) -> p c b", b=B)
        from_block = lambda ap: ap.rearrange("p (c r) -> p c r", r=QD)[:, :, 0:B]

        block = ctx.enter_context(nc.Block())

        @block.sync
        def _(sp):
            nat = lambda w: w.rearrange("(k p) n -> p k n", p=P)
            sp.dma_start(xb[:], x[0].rearrange("(t p) f -> p t f", p=P)).then_inc(ld_x, 16)
            sp.dma_start(wemb, nat(W_emb)).then_inc(ld_emb, 16)
            sp.wait_ge(ld_emb, 16)
            sp.dma_start(wqkv[:], nat(W_qkv)).then_inc(ld_wqkv, 16)
            with sp.Fori(0, B) as b:
                sp.wait_ge(s["xT_ready"], sp.snap(b * KT + KT))
                sp.dma_start(xb[:], x[bass.ds((b + 1) % B, 1), :, :].rearrange("o (t p) f -> p (o t) f", p=P)).then_inc(ld_x, 16)
            sp.wait_ge(s["xr_ready"], (B + 1) * TT)
            sp.dma_start(brz2, b_hh[0:2 * D].partition_broadcast(P)).then_inc(ld_bias2, 16)
            sp.dma_start(gi[:, 2 * D:3 * D], b_hh[2 * D:3 * D].partition_broadcast(P)).then_inc(ld_bias2, 16)
            with sp.Fori(0, T // BLK) as m:
                sp.wait_ge(s["outrow_ready"], sp.snap(m + 3))
                for b in range(B):
                    sp.dma_start(out[b, bass.ds(m * BLK, BLK), :], out_rows[BLK * b:BLK * b + BLK, :]).then_inc(st_out, 16)
                sp.wait_ge(st_out, sp.snap(m * (16 * B) + 16 * B))
                sp.sem_inc(s["out_sent"], 1)
            sp.wait_ge(st_out, 16 * B * T // BLK)

        @block.gpsimd
        def _(pool):
            def await_on_pool(semaphore, value):
                pool.wait_ge(semaphore, value)
                pool.sem_inc(s["pool_waited"], 1)

            nc.gpsimd.memset(ident[:], 0.0).then_inc(s["ident_zero"], 1)
            pool.wait_ge(s["ident_zero"], 1)
            nc.gpsimd.affine_select(out=ident[:], in_=ident[:], compare_op=ALU.not_equal, fill=1.0, base=0,
                                    pattern=[[-1, P]], channel_multiplier=1).then_inc(s["ident_ready"], 1)
            nc.gpsimd.memset(half_neg[:], -0.5).then_inc(s["half_ready"], 1)

            def rms_of_rows(batch):
                await_on_pool(s["ssq_done"], pool.snap(batch + 1))
                nc.gpsimd.tensor_scalar(ms[:], ssq[:], D * EPS, None, ALU.add).then_inc(s["ms_done"], 1)
                await_on_pool(s["ms_done"], pool.snap(batch + 1))
                nc.gpsimd.tensor_tensor(rstd[:], ms[:], half_neg[:, 0:TT], ALU.pow).then_inc(s["rstd_done"], 1)

            await_on_pool(s["half_ready"], 1)
            rms_of_rows(0)
            pool.dma_start(wout[:], W_out.rearrange("(k p) n -> p k n", p=P)).then_inc(ld_wout, 16)
            pool.dma_start(wih[:], W_ih.rearrange("(k p) n -> p k n", p=P)).then_inc(ld_wih, 16)
            pool.dma_start(binT[:], b_ih[2 * D:3 * D].rearrange("(k p) -> p k", p=P),
                           allow_slow_non_contiguous=True).then_inc(ld_bias, 16)
            pool.dma_start(brz[:], b_ih[0:2 * D].partition_broadcast(P)).then_inc(ld_bias, 16)
            await_on_pool(s["gk_ready"], 1)
            with pool.Fori(0, B) as b:
                for n in range(N_TILES):
                    n1 = pool.snap(b * N_TILES + (n + 1))
                    await_on_pool(s["ss_done"], n1)
                    nc.gpsimd.tensor_scalar(qk_ms[:, n % 2], qk_ss[:, n % 2], DH * EPS, None, ALU.add).then_inc(s["qkms_done"], 1)
                    await_on_pool(s["qkms_done"], n1)
                    nc.gpsimd.tensor_tensor(qk_rs[:, n % 2], qk_ms[:, n % 2], half_neg[:], ALU.pow).then_inc(s["qkrs_done"], 1)
                    await_on_pool(s["qkrs_done"], n1)
                    nc.gpsimd.tensor_tensor(norm_qk[:, n % 2].rearrange("p (h d) -> p h d", d=DH),
                                            g_row[:].rearrange("p a h d -> p (a h) d"),
                                            qk_rs[:, n % 2, :].unsqueeze(2).broadcast_to([P, 8, DH]), ALU.mult).then_inc(s["norm_done"], 1)
                rms_of_rows(b + 1)
                await_on_pool(s["oT_ready"], pool.snap(b * G + (G + 1)))
                await_on_pool(s["xT_ready"], pool.snap(b * KT + KT))
                nc.gpsimd.tensor_tensor(xT[:].rearrange("p k t -> p (k t)"), xT[:].rearrange("p k t -> p (k t)"),
                                        oT[:].rearrange("p k t -> p (k t)"), ALU.add).then_inc(s["ox_ready"], 1)

            await_on_pool(s["proj_done"], B * N_TILES)
            pool.dma_start(whh[:], W_hh.rearrange("(k p) n -> p k n", p=P)).then_inc(ld_whh, 16)
            def copy_x1(first):
                nc.gpsimd.tensor_copy(x1_blk.rearrange("p c (b t) -> p (c b) t", b=B),
                                      x1T[:].rearrange("p c b t -> p (c b) t")[:, :, bass.ds(first, BLK)]
                                      ).then_inc(s["x1blk_ready"], 1)

            for c in range(KT):
                await_on_pool(s["x1_ready"], B * KT + c + 1)
                first_copy = nc.gpsimd.tensor_copy(x1_blk[:, c, :].rearrange("p (b t) -> p b t", b=B), x1T[:, c, :, 0:BLK])
            first_copy.then_inc(s["x1blk_ready"], 1)
            await_on_pool(s["gi_done"], 1)
            copy_x1(BLK)
            with pool.Fori(0, T // BLK) as m:
                await_on_pool(s["gi_done"], pool.snap(m + 2))
                copy_x1((m + 2) % (T // BLK) * BLK)
                await_on_pool(s["outblk_done"], pool.snap(m * BLK + BLK))
                await_on_pool(s["outT_done"], pool.snap(m + 1))
                nc.gpsimd.tensor_copy(out_full, out_blk.rearrange("p u r -> p (u r)")).then_inc(s["outfull_ready"], 1)

        @block.tensor
        def _(pe):
            def transpose(dst, src):
                return nc.tensor.transpose(dst, src, ident[:])

            pe.wait_ge(ld_cond, 16 * (KT + 2))
            pe.wait_ge(ld_emb, 16)
            pe.wait_ge(s["pm_zero"], 1)
            for k in range(KT):
                for j in range(4):
                    last = nc.tensor.matmul(ps[QD * j:QD * j + B, PM, 0:2 * P], condT[:, k, :],
                                            wemb[:, k, :].rearrange("p (c j x) -> p c j x", c=2 * KT, j=4)[:, :, j, :],
                                            start=(k == 0), stop=(k == KT - 1), tile_position=(0, QD * j))
            last.then_inc(s["emb_done"], 1)
            pe.wait_ge(s["ident_ready"], 1)
            pe.wait_ge(s["identr_ready"], 1)
            pe.wait_ge(s["mod_ready"], 1)

            with pe.Fori(0, B) as b:
                for c in range(KT):
                    pe.wait_ge(s["x1_ready"], pe.snap(b * KT + (c + 1)))
                    for t in range(TT):
                        if c == 0:
                            pe.wait_ge(s["xr_ready"], pe.snap(b * TT + (t + 1)))
                        last = transpose(ps[:, SC[c], P * t:P * t + P], xr[:, t, P * c:P * c + P])
                    last.then_inc(s["xn_ps"], 1)
                for c in range(KT):
                    for t in range(TT):
                        last = transpose(ps[:, X_BANKS[c], P * t:P * t + P], xb[:, t, P * c:P * c + P])
                    last.then_inc(s["x_ps"], 1)
                pe.wait_ge(ld_wqkv, 16)

                def transpose_stack(qk, i, bank):
                    for hh in range(4):
                        last = nc.tensor.transpose(ps[:, bank, P * hh:P * hh + P].bitcast(F32R),
                                                   split[:, qk, hh].rearrange("p c d -> p (c d)"), ident_r[:])
                    last.then_inc(s[("tq_done", "tk_done")[qk]], 1)

                for slot in range(N_SLOTS):
                    n, i, m = slot, slot - 2, slot - LAG

                    def transpose_rexp():
                        pe.wait_ge(s["rexp_done"], pe.snap(b * N_QUADS + m))
                        transpose(ps[:, PJ[slot % 2], 3 * P:4 * P], rexp[:]).then_inc(s["rtr_done"], 1)

                    def project(k):
                        g, t = divmod(n, TT)
                        return nc.tensor.matmul(ps[:, pj(n), 0:3 * P], xnT[:, k, P * t:P * t + P],
                                                wqkv[:, k, :].rearrange("p (a g n) -> p a g n", a=3, g=G)[:, :, g, :],
                                                start=(k == 0), stop=(k == KT - 1))

                    def transpose_q():
                        pe.wait_ge(s["kT_ready"], pe.snap(b * N_TILES + i))
                        pe.wait_ge(s["split_ready"], pe.snap(b * N_TILES + (i + 1)))
                        transpose_stack(0, i, PM)

                    if slot > LAG and i < N_TILES:
                        transpose_q()
                    if 0 <= m - 1 and (i < N_TILES or m == N_QUADS):
                        transpose_rexp()
                    if 0 <= m < N_QUADS:
                        g, q = divmod(m, TT)
                        if q == 0:
                            pe.wait_ge(s["kT_ready"], pe.snap(b * N_TILES + (TT * g + TT)))
                        for hh in range(4):
                            if m == 0:
                                pass
                            elif hh < 2:
                                pe.wait_ge(s["ptev_dve"], pe.snap(b * (2 * N_QUADS) + (2 * m - 1 + hh)))
                            else:
                                pe.wait_ge(s["ptev_act"], pe.snap(b * (2 * N_QUADS) + (2 * m - 3 + hh)))
                            nc.tensor.matmul(ps[:, SC[hh], :], stacks[:, g % 2, 0, hh, P * q:P * q + P], stacks[:, g % 2, 1, hh, :],
                                             start=True, stop=True).then_inc(s["s_done"], 1)
                            if hh == 0 and i >= N_TILES:
                                transpose_rexp()

                    if slot == LAG:
                        transpose_q()
                    if 0 <= m - 1 < N_QUADS:
                        g, q = divmod(m - 1, TT)
                        if q == 0:
                            pe.wait_ge(s["oT_ready"], pe.snap(b * G + (g + 1)))
                        pe.wait_ge(s["ptev_dve"], pe.snap(b * (2 * N_QUADS) + 2 * m))
                        pe.wait_ge(s["ptev_act"], pe.snap(b * (2 * N_QUADS) + 2 * m))
                        for kc in range(TT):
                            for hh in range(4):
                                last = nc.tensor.matmul(
                                    ps[QD * hh:QD * hh + QD, PO, P * q:P * q + P],
                                    v_sb[:, g, kc, QD * hh:QD * hh + QD], probsT[:, hh, kc, :],
                                    start=(kc == 0), stop=(kc == TT - 1), tile_position=(0, QD * hh))
                        last.then_inc(s["pv_done"], 1)

                    if slot >= LAG and i < N_TILES:
                        pe.wait_ge(s["qT_ready"], pe.snap(b * N_TILES + (i + 1)))
                        transpose_stack(1, i, PM)
                    if n < N_TILES:
                        if n == 0:
                            pe.wait_ge(s["xnT_dve"], pe.snap(b * 2 + 2))
                            pe.wait_ge(s["xnT_act"], pe.snap(b * 2 + 2))
                        if n >= 4:
                            if n >= 6:
                                pe.wait_ge(s["qn_done"], pe.snap(b * N_TILES + (n - 1)))
                            else:
                                pe.wait_ge(s["xT_ready"], pe.snap(b * KT + KT))
                        if 0 <= m - 1:
                            pe.wait_ge(s["r_ready"], pe.snap(b * N_QUADS + m))
                        project(0)
                    for hh in range(4):
                        if 0 <= m < N_QUADS:
                            pe.wait_ge(s["exp_done"], pe.snap(b * (4 * N_QUADS) + (4 * m + hh + 1)))
                            for kc in range(TT):
                                last = transpose(ps[:, SC[hh], P * kc:P * kc + P], probs[:, hh, P * kc:P * kc + P])
                            last.then_inc(s["pt_done"], 1)
                        if n < N_TILES and hh == 1:
                            project(1)
                    if n < N_TILES:
                        project(2)
                        project(3).then_inc(s["proj_done"], 1)
                    if slot < LAG and 0 <= i:
                        if i == 0:
                            pe.wait_ge(s["xT_ready"], pe.snap(b * KT + KT))
                        else:
                            pe.wait_ge(s["kT_ready"], pe.snap(b * N_TILES + i))
                        pe.wait_ge(s["split_ready"], pe.snap(b * N_TILES + (i + 1)))
                        transpose_stack(0, i, PM)
                        transpose_stack(1, i, PO)
                pe.wait_ge(ld_wout, 16)
                pe.wait_ge(s["oT_ready"], pe.snap(b * G + (G + 1)))
                for c in range(KT):
                    for k in range(KT):
                        last = nc.tensor.matmul(ps[:, SC[c], :], wout[:, k, P * c:P * c + P], oT[:, k, :],
                                                start=(k == 0), stop=(k == KT - 1))
                    last.then_inc(s["y_done"], 1)

            pe.wait_ge(ld_wih, 16)
            pe.wait_ge(ld_whh, 16)

            WIDE = [(gate, lo, lo + 192, k) for gate in range(2) for lo in (0, 192) for k in range(KT)]
            NARROW_RZ = [(gate, 384, D, k) for gate in range(2) for k in range(KT)]
            N_GATE = [(2, P * c, P * c + P, k) for c in range(KT) for k in range(KT)]
            narrow = NARROW_RZ + N_GATE
            N_SINGLE = 2 * (BLK - 1 - len(WIDE)) - len(narrow)
            PIECES_OF_STEP = ([[piece] for piece in WIDE]
                              + [narrow[2 * i:2 * i + 2] for i in range((len(narrow) - N_SINGLE) // 2)]
                              + [[piece] for piece in narrow[len(narrow) - N_SINGLE:]])

            def gi_pieces(pieces):
                for gate, lo, hi, k in pieces:
                    weights = wih[:, k, D * gate + lo:D * gate + hi]
                    lhsT, rhs = (weights, x1_blk[:, k, :]) if gate == 2 else (x1_blk[:, k, :], weights)
                    last = nc.tensor.matmul(ps[:, (GR, GZ, GN)[gate], lo:hi], lhsT, rhs, start=(k == 0), stop=(k == KT - 1))
                return last

            def inject(bank, width, gates, u):
                for j in range(4):
                    last = nc.tensor.matmul(ps[QD * j:QD * j + B, bank, 0:width], ident[:, u::BLK], gate_cols(gi, gates, j),
                                            start=True, stop=False, tile_position=(0, QD * j))
                return last

            def add_hidden_side(bank, width, gates, prev):
                for k in range(KT):
                    for j in range(4):
                        last = nc.tensor.matmul(ps[QD * j:QD * j + B, bank, 0:width], prev[:, B * k:B * k + B],
                                                gate_cols(whh[:, k, :], gates, j), start=False, stop=(k == KT - 1),
                                                tile_position=(0, QD * j))
                return last

            R_AND_N, Z_ONLY = slice(0, 3, 2), 1

            def output_rows():
                for c in range(KT):
                    last = transpose(ps[:, PH, P * c:P * c + P], out_full[:, P * c:P * c + P])
                return last

            pe.wait_ge(s["x1blk_ready"], 1)
            gi_pieces(WIDE + narrow).then_inc(s["gi_done"], 1)
            pe.wait_ge(s["gi_ready"], 1)
            pe.wait_ge(ld_bias2, 16 * 2)
            pe.wait_ge(s["qT_done"], 1)
            inject(RQ, 2 * P, R_AND_N, 0)
            pe.wait_ge(s["zT_done"], 1)
            inject(Z, P, Z_ONLY, 0).then_inc(s["inject_done"], 1)
            with pe.Fori(0, T // BLK) as m:
                for u in range(BLK):
                    t1 = pe.snap(m * BLK + (u + 1))
                    t2 = pe.snap(m * BLK + (u + 2))
                    pe.wait_ge(s["h_ready"], t1)
                    add_hidden_side(RQ, 2 * P, R_AND_N, state[:, (u - 1) % 2, :]).then_inc(s["rq_done"], 1)
                    add_hidden_side(Z, P, Z_ONLY, state[:, (u - 1) % 2, :]).then_inc(s["z_done"], 1)
                    if u == BLK - 1:
                        pe.wait_ge(s["gi_ready"], pe.snap(m + 2))
                    pe.wait_ge(s["qT_done"], t2)
                    inject(RQ, 2 * P, R_AND_N, (u + 1) % BLK)
                    if u == 0:
                        pe.wait_ge(s["x1blk_ready"], pe.snap(m + 2))
                        pe.wait_ge(s["gin_ready"], pe.snap(m + 1))
                    if u < BLK - 1:
                        last = gi_pieces(PIECES_OF_STEP[u])
                    if u == BLK - 2:
                        last.then_inc(s["gi_done"], 1)
                    pe.wait_ge(s["zT_done"], t2)
                    inject(Z, P, Z_ONLY, (u + 1) % BLK).then_inc(s["inject_done"], 1)
                    if u == OUT_STEP:
                        pe.wait_ge(s["outfull_ready"], pe.snap(m + 1))
                        pe.wait_ge(s["outrow_ready"], pe.snap(m + 1))
                        output_rows().then_inc(s["outT_done"], 1)
            pe.wait_ge(s["outfull_ready"], T // BLK + 1)
            pe.wait_ge(s["outrow_ready"], T // BLK + 1)
            output_rows().then_inc(s["outT_done"], 1)

        @block.scalar
        def _(act):
            for k in range(KT):
                act.dma_start(condT[:, k, :], cond[:, P * k:P * k + P].rearrange("b p -> p b"),
                             allow_slow_non_contiguous=True).then_inc(ld_cond, 16)
            act.dma_start(bembT[:], b_emb.rearrange("(k p) -> p k", p=P), allow_slow_non_contiguous=True).then_inc(ld_cond, 16)
            act.dma_start(gnT[:], g_norm.rearrange("(k p) -> p k", p=P), allow_slow_non_contiguous=True).then_inc(ld_cond, 16)
            for hh in range(4):
                act.dma_start(g_row[:, 0, hh, :], g_q.partition_broadcast(P)).then_inc(ld_g, 16)
                act.dma_start(g_row[:, 1, hh, :], g_k.partition_broadcast(P)).then_inc(ld_g, 16)

            def sum_squares():
                for t in range(TT):
                    last = nc.scalar.activation(xr[:, t, :], xb[:, t, :], ACT.Square, accum_out=ssq[:, t:t + 1])
                last.then_inc(s["ssq_done"], 1)

            act.wait_ge(ld_x, 16)
            sum_squares()
            act.wait_ge(ld_g, 128)
            nc.scalar.mul(g_row[:, 1], g_row[:, 1], DH ** 0.5).then_inc(s["gk_ready"], 1)
            with act.Fori(0, B) as b:
                act.wait_ge(s["modb_ready"], act.snap(b + 1))
                for c in (1, 3):
                    act.wait_ge(s["xn_ps"], act.snap(b * KT + (c + 1)))
                    nc.scalar.activation(xnT[:, c, :], ps[:, SC[c], :], ACT.Identity, bias=mod_b[:, KT + c:KT + c + 1],
                                         scale=mod_b[:, c:c + 1]).then_inc(s["xnT_act"], 1)
                for c in range(KT):
                    act.wait_ge(s["x_ps"], act.snap(b * KT + (c + 1)))
                    if c == 0:
                        act.wait_ge(s["x1_ready"], act.snap(b * KT + KT))
                    nc.scalar.activation(xT[:, c, :], ps[:, X_BANKS[c], :], ACT.Copy).then_inc(s["xT_ready"], 1)
                for slot in range(N_SLOTS):
                    j, i, m = slot - 1, slot - 2, slot - LAG
                    if 0 <= j < N_TILES:
                        g, t = divmod(j, TT)
                        act.wait_ge(s["proj_done"], act.snap(b * N_TILES + (j + 1)))
                        nc.scalar.activation(v_sb[:, g, t, :], ps[:, pj(j), 2 * P:3 * P], ACT.Copy)
                        if j >= 2:
                            act.wait_ge(s["ss_done"], act.snap(b * N_TILES + (j - 1)))
                        nc.scalar.activation(sq[:, j % 2, :], ps[:, pj(j), 0:2 * P], ACT.Square).then_inc(s["sq_done"], 1)

                    def evacuate_stack(qk, i, bank):
                        g, t = divmod(i, TT)
                        act.wait_ge(s[("tq_done", "tk_done")[qk]], act.snap(b * N_TILES + (i + 1)))
                        nc.scalar.activation(stacks[:, g % 2, qk, :, P * t:P * t + P],
                                             ps[:, bank, :].rearrange("p (h t) -> p h t", h=4),
                                             ACT.Copy).then_inc(s[("qT_ready", "kT_ready")[qk]], 1)

                    if 3 <= slot <= LAG:
                        evacuate_stack(0, slot - 3, PM)
                        evacuate_stack(1, slot - 3, PO)
                    if slot >= LAG and i < N_TILES:
                        evacuate_stack(0, i, PM)
                    if 0 <= m - 1 < N_QUADS:
                        g, q = divmod(m - 1, TT)
                        act.wait_ge(s["rtr_done"], act.snap(b * N_QUADS + m))
                        nc.scalar.activation(rT_sb[:, g % 2, P * q:P * q + P], ps[:, PJ[slot % 2], 3 * P:4 * P],
                                             ACT.Copy).then_inc(s["r_ready"], 1)
                    if 0 <= m < N_QUADS:
                        for hh in range(4):
                            if hh == 2 and i < N_TILES:
                                evacuate_stack(1, i, PM)
                            act.wait_ge(s["max_done"], act.snap(b * (4 * N_QUADS) + (4 * m + hh + 1)))
                            nc.scalar.activation(probs[:, hh, :], ps[:, SC[hh], :], ACT.Exp,
                                                 bias=negmax[:, m % 2, hh:hh + 1],
                                                 accum_out=sums[:, m % 2, hh:hh + 1]).then_inc(s["exp_done"], 1)
                        for hh in (2, 3):
                            act.wait_ge(s["pt_done"], act.snap(b * (4 * N_QUADS) + (4 * m + hh + 1)))
                            nc.scalar.activation(probsT[:, hh, :, :].rearrange("p k q -> p (k q)"), ps[:, SC[hh], :],
                                                 ACT.Copy).then_inc(s["ptev_act"], 1)
                act.wait_ge(ld_x, act.snap(b * 16 + 32))
                sum_squares()

            act.wait_ge(ld_bias, 16 * 2)
            def evacuate_gi_n():
                for c in range(KT):
                    last = nc.scalar.activation(gi_nT[:, :, B * c:B * c + B].rearrange("p t b -> p b t"),
                                                ps[:, GN, P * c:P * c + P].rearrange("p (b t) -> p b t", b=B),
                                                ACT.Identity, bias=binT[:, c:c + 1])
                return last

            def evacuate_rows():
                return nc.scalar.activation(out_rows, ps[:, PH, :], ACT.Copy)

            act.wait_ge(s["gi_done"], 1)
            evacuate_gi_n().then_inc(s["gin_ready"], 1)
            with act.Fori(0, T // BLK) as m:
                for u in range(BLK):
                    t1 = act.snap(m * BLK + (u + 1))
                    t2 = act.snap(m * BLK + (u + 2))
                    act.wait_ge(s["rT_done"], t1)
                    nc.scalar.activation(b4(t_r[:]), from_block(rT_ps), ACT.Tanh, scale=0.5).then_inc(s["tr_done"], 1)
                    act.wait_ge(s["v_done"], t1)
                    nc.scalar.activation(n_new[:], v_ps, ACT.Tanh).then_inc(s["n_done"], 1)
                    act.wait_ge(s["zT_done"], t2)
                    nc.scalar.activation(b4(t_z[:]), from_block(zT_ps), ACT.Tanh, scale=0.5).then_inc(s["tz_done"], 1)
                act.wait_ge(s["gi_done"], act.snap(m + 2))
                evacuate_gi_n().then_inc(s["gin_ready"], 1)
                act.wait_ge(s["outT_done"], act.snap(m + 1))
                act.wait_ge(s["out_sent"], act.snap(m + 1))
                evacuate_rows().then_inc(s["outrow_ready"], 1)
            act.wait_ge(s["outT_done"], T // BLK + 1)
            act.wait_ge(s["out_sent"], T // BLK + 1)
            evacuate_rows().then_inc(s["outrow_ready"], 1)

        @block.vector
        def _(dve):
            prime = (("x1_ready", KT), ("oT_ready", 1), ("outrow_ready", 1), ("out_sent", 2))
            for name, count in prime:
                dve.sem_inc(s[name], count)
            def over_rms(batch):
                dve.wait_ge(s["rstd_done"], dve.snap(batch + 1))
                for t in range(TT):
                    nc.vector.tensor_scalar(xr[:, t, :], xb[:, t, :], rstd[:, t:t + 1], None, ALU.mult).then_inc(s["xr_ready"], 1)

            nc.vector.memset(ps[:, PM, :], 0.0).then_inc(s["pm_zero"], 1)
            dve.wait_ge(s["ident_ready"], 1)
            nc.vector.tensor_copy(ident_r[:], ident[:]).then_inc(s["identr_ready"], 1)
            dve.wait_ge(ld_cond, 16 * (KT + 2))
            nc.vector.tensor_scalar_add(bembT[:, 0:KT], bembT[:, 0:KT], 1.0).then_inc(s["bemb1"], 1)
            nc.vector.tensor_scalar_mul(gnT[:], gnT[:], D ** 0.5).then_inc(s["gn_ready"], 1)
            over_rms(0)
            dve.wait_ge(s["emb_done"], 1)
            nc.vector.transpose(embT, ps[:, PM, 0:2 * P]).then_inc(s["embT_done"], 1)
            dve.wait_ge(s["embT_done"], 1)
            dve.wait_ge(s["bemb1"], 1)
            dve.wait_ge(s["gn_ready"], 1)
            for c in range(KT):
                nc.vector.tensor_scalar(mod_all[:, :, c], embT[:, QD * c:QD * c + B], bembT[:, c:c + 1], gnT[:, c:c + 1],
                                        ALU.add, ALU.mult)
                last = nc.vector.tensor_scalar(mod_all[:, :, KT + c], embT[:, QD * (KT + c):QD * (KT + c) + B],
                                               bembT[:, KT + c:KT + c + 1], None, ALU.add)
            last.then_inc(s["mod_ready"], 1)
            dve.wait_ge(s["mod_ready"], 1)
            with dve.Fori(0, B) as b:
                nc.vector.tensor_copy(mod_b[:].rearrange("p (o n) -> p o n", o=1),
                                      mod_all[:, bass.ds(b, 1), :]).then_inc(s["modb_ready"], 1)
                dve.wait_ge(s["modb_ready"], dve.snap(b + 1))
                for c in (0, 2):
                    dve.wait_ge(s["xn_ps"], dve.snap(b * KT + (c + 1)))
                    nc.vector.tensor_scalar(xnT[:, c, :], ps[:, SC[c], :], mod_b[:, c:c + 1], mod_b[:, KT + c:KT + c + 1],
                                            ALU.mult, ALU.add).then_inc(s["xnT_dve"], 1)

                def over_qk_rms(j):
                    j1 = dve.snap(b * N_TILES + (j + 1))
                    dve.wait_ge(s["norm_done"], j1)
                    nc.vector.tensor_tensor(qn[:, j % 2, :], ps[:, pj(j), 0:2 * P], norm_qk[:, j % 2, :], ALU.mult).then_inc(s["qn_done"], 1)
                    q, k = (qn[:, j % 2, P * a:P * a + P].rearrange("p (h d) -> p h d", d=DH).unsqueeze(2).broadcast_to([P, 4, 2, DH])
                            for a in range(2))
                    q_high, q_low = split[:, 0, :, 0:2, :], split[:, 0, :, 2:4, :]
                    k_high, k_low = split[:, 1, :, 0::2, :], split[:, 1, :, 1::2, :]
                    if j > 0:
                        dve.wait_ge(s["tk_done"], dve.snap(b * N_TILES + j))
                    dve.wait_ge(s["qn_done"], j1)
                    nc.vector.tensor_copy(q_high, q).then_inc(s["high_done"], 1)
                    nc.vector.tensor_copy(k_high, k).then_inc(s["high_done"], 1)
                    dve.wait_ge(s["high_done"], dve.snap(b * (2 * N_TILES) + (2 * j + 2)))
                    nc.vector.tensor_tensor(q_low, q, q_high.bitcast(F32), ALU.subtract)
                    nc.vector.tensor_tensor(k_low, k, k_high.bitcast(F32), ALU.subtract).then_inc(s["split_ready"], 1)

                for slot in range(N_SLOTS):
                    j, m = slot - 1, slot - LAG
                    if 0 <= j < N_TILES:
                        dve.wait_ge(s["sq_done"], dve.snap(b * N_TILES + (j + 1)))
                        nc.vector.reduce_sum(qk_ss[:, j % 2, :], sq[:, j % 2, :].rearrange("p (h d) -> p h d", d=DH),
                                             AX_X).then_inc(s["ss_done"], 1)
                    if 2 <= slot <= LAG:
                        over_qk_rms(j - 1)
                    if 0 <= m < N_QUADS:
                        for hh in range(4):
                            dve.wait_ge(s["s_done"], dve.snap(b * (4 * N_QUADS) + (4 * m + hh + 1)))
                            nc.vector.reduce_max(negmax[:, m % 2, hh:hh + 1], ps[:, SC[hh], :], AX_X,
                                                 negate=True).then_inc(s["max_done"], 1)
                        for hh in (0, 1):
                            dve.wait_ge(s["pt_done"], dve.snap(b * (4 * N_QUADS) + (4 * m + hh + 1)))
                            nc.vector.tensor_copy(probsT[:, hh, :, :].rearrange("p k q -> p (k q)"),
                                                  ps[:, SC[hh], :]).then_inc(s["ptev_dve"], 1)
                        dve.wait_ge(s["exp_done"], dve.snap(b * (4 * N_QUADS) + (4 * m + 4)))
                        nc.vector.reciprocal(recip[:], sums[:, m % 2, :]).then_inc(s["recip_done"], 1)
                    if LAG <= slot and j < N_TILES:
                        over_qk_rms(j)
                    if 0 <= m < N_QUADS:
                        dve.wait_ge(s["recip_done"], dve.snap(b * N_QUADS + (m + 1)))
                        if m > 0:
                            dve.wait_ge(s["rtr_done"], dve.snap(b * N_QUADS + m))
                        nc.vector.tensor_copy(rexp[:].rearrange("p (h d) -> p h d", d=DH),
                                              recip[:].unsqueeze(2).broadcast_to([P, 4, DH])).then_inc(s["rexp_done"], 1)
                    if 0 <= m - 1 < N_QUADS and (m - 1) % TT == TT - 1:
                        dve.wait_ge(s["pv_done"], dve.snap(b * N_QUADS + m))
                        dve.wait_ge(s["r_ready"], dve.snap(b * N_QUADS + m))
                        nc.vector.tensor_tensor(oT[:, (m - 1) // TT, :], ps[:, PO, :], rT_sb[:, (m - 1) // TT % 2, :], ALU.mult).then_inc(s["oT_ready"], 1)
                over_rms(b + 1)
                dve.wait_ge(s["ox_ready"], dve.snap(b + 1))
                for c in range(KT):
                    dve.wait_ge(s["y_done"], dve.snap(b * KT + (c + 1)))
                    nc.vector.tensor_tensor(x1T[:, c, bass.ds(b, 1), :], ps[:, SC[c]:SC[c] + 1, :], xT[:, c:c + 1, :],
                                            ALU.add).then_inc(s["x1_ready"], 1)

            dve.wait_ge(s["x1_ready"], (B + 1) * KT)
            dve.wait_ge(ld_bias, 16 * 2)
            dve.wait_ge(ld_bias2, 16 * 2)
            nc.vector.tensor_tensor(brz[:], brz[:], brz2, ALU.add).then_inc(s["brz_ready"], 1)
            nc.vector.memset(ps[:, RQ, :], 0.0).then_inc(s["qT_done"], 1)
            nc.vector.memset(out_full, 0.0).then_inc(s["outfull_ready"], 1)
            nc.vector.memset(ps[:, Z, :], 0.0).then_inc(s["zT_done"], 1)
            nc.vector.tensor_copy(state[:, 1, :], condT[:].rearrange("p k b -> p (k b)")).then_inc(s["h_ready"], 1)
            dve.wait_ge(s["brz_ready"], 1)

            def evacuate_gi_rz():
                nc.vector.tensor_tensor(gi[:, 0:D], ps[:, GR, :], brz[:, 0:D], ALU.add)
                return nc.vector.tensor_tensor(gi[:, D:2 * D], ps[:, GZ, :], brz[:, D:2 * D], ALU.add)

            dve.wait_ge(s["gi_done"], 1)
            evacuate_gi_rz().then_inc(s["gi_ready"], 1)
            dve.wait_ge(s["h_ready"], 1)
            with dve.Fori(0, T // BLK) as m:
                for u in range(BLK):
                    t1 = dve.snap(m * BLK + (u + 1))
                    t2 = dve.snap(m * BLK + (u + 2))
                    prev, new = state[:, (u - 1) % 2, :], state[:, u % 2, :]
                    if u == BLK - 1:
                        dve.wait_ge(s["inject_done"], t1)
                        dve.wait_ge(s["gi_done"], dve.snap(m + 2))
                        evacuate_gi_rz().then_inc(s["gi_ready"], 1)
                    dve.wait_ge(s["rq_done"], t1)
                    nc.vector.transpose(rT_ps, ps[:, RQ, 0:P]).then_inc(s["rT_done"], 1)
                    nc.vector.transpose(qT[:], ps[:, RQ, P:2 * P]).then_inc(s["qT_done"], 1)
                    if u == 0:
                        dve.wait_ge(s["gin_ready"], dve.snap(m + 1))
                    dve.wait_ge(s["tr_done"], t1)
                    dve.wait_ge(s["qT_done"], t2)
                    nc.vector.scalar_tensor_tensor(out=b4(w_n[:]), in0=b4(t_r[:]), scalar=1.0, in1=from_block(qT[:]),
                                                   op0=ALU.add, op1=ALU.mult).then_inc(s["w_done"], 1)
                    dve.wait_ge(s["w_done"], t1)
                    nc.vector.scalar_tensor_tensor(out=v_ps, in0=w_n[:], scalar=0.5, in1=gi_nT[:, u, :],
                                                   op0=ALU.mult, op1=ALU.add).then_inc(s["v_done"], 1)
                    dve.wait_ge(s["z_done"], t1)
                    nc.vector.transpose(zT_ps, ps[:, Z, 0:P]).then_inc(s["zT_done"], 1)
                    dve.wait_ge(s["n_done"], t1)
                    nc.vector.tensor_tensor(h_minus_n[:], prev, n_new[:], ALU.subtract)
                    nc.vector.tensor_tensor(n_plus_h[:], n_new[:], prev, ALU.add).then_inc(s["sd_done"], 1)
                    dve.wait_ge(s["sd_done"], t1)
                    nc.vector.memset(wait_mark[:], 0.0)
                    dve.wait_ge(s["tz_done"], t1)
                    nc.vector.scalar_tensor_tensor(out=z_part[:], in0=h_minus_n[:], scalar=0.5, in1=t_z[:],
                                                   op0=ALU.mult, op1=ALU.mult).then_inc(s["zp_done"], 1)
                    dve.wait_ge(s["zp_done"], t1)
                    nc.vector.scalar_tensor_tensor(out=new, in0=n_plus_h[:], scalar=0.5, in1=z_part[:],
                                                   op0=ALU.mult, op1=ALU.add).then_inc(s["h_ready"], 1)
                    dve.wait_ge(s["h_ready"], t2)
                    if u == 0:
                        dve.wait_ge(s["outfull_ready"], dve.snap(m + 1))
                    nc.vector.tensor_tensor(out_blk[:, :, u:u + 1], new.unsqueeze(2),
                                            x1T[:].rearrange("p c b t -> p (c b) t")[:, :, bass.ds(m * BLK + u, 1)],
                                            ALU.add).then_inc(s["outblk_done"], 1)


_INS = ["x", "cond_2048", "L0_cond_W_emb", "L0_cond_b_emb", "L0_cond_g_norm", "L0_cond_W_qkv", "L0_cond_g_q",
        "L0_cond_g_k", "L0_cond_W_out", "L1_cond_W_ih", "L1_cond_W_hh", "L1_cond_b_ih", "L1_cond_b_hh"]


def kernel(**inputs):
    import numpy as _np
    import concourse.bacc as _bacc
    from concourse import mybir as _mybir
    from concourse.bass_utils import run_bass_kernel_spmd as _run

    nc = _bacc.Bacc("TRN2", target_bir_lowering=False, num_devices=1)
    arrays, args = {}, []
    for name in _INS:
        a = _np.ascontiguousarray(inputs[name])
        arrays[f"in_{name}"] = a
        args.append(nc.dram_tensor(f"in_{name}", a.shape, _mybir.dt.from_np(a.dtype), kind="ExternalInput").ap())
    args.append(nc.dram_tensor("out_0", (B, T, D), F32, kind="ExternalOutput").ap())
    attention_gru_kernel(nc, *args)
    r = _run(nc, [arrays], core_ids=[0])
    return r.results[0]["out_0"]
```
